# Optimizing a Trainium2 kernel written in Bass

```python
import numpy as np
import jax
import jax.numpy as jnp

def _softmax(x, axis=-1):
    return jax.nn.softmax(x, axis=axis)

def _gelu(x):
    return jax.nn.gelu(x, approximate=True)

def _silu(x):
    return jax.nn.silu(x)

def _sigmoid(x):
    return jax.nn.sigmoid(x)

def _layernorm(x, axis=-1, eps=1e-05):
    m = jnp.mean(x, axis=axis, keepdims=True)
    v = jnp.var(x, axis=axis, keepdims=True)
    return (x - m) / jnp.sqrt(v + eps)

def _scatter_add(tgt, idx, src, axis=0):
    return tgt.at[idx].add(src)

def _segment_sum(src, seg, n):
    return jax.ops.segment_sum(src, seg, n)
kernel_name = 'mk_vit_tower_d1_tok_img768_r4_696f25'

def setup_inputs(seed: int=0):
    np.random.seed(seed)
    _w = jnp.asarray

    def _rec_inputs():
        import jax
        import jax.numpy as jnp
        _rk = jax.random.key(seed)
        x = -0.000596345 + 1.00056 * jax.random.normal(jax.random.fold_in(_rk, 1), (2, 3, 64, 64), jnp.float32)
        return x
    x = _rec_inputs()

    def _L0_tok_setup():
        import jax, jax.numpy as jnp
        import numpy as np
        B = 16
        IMG = 64
        CH = 3
        EMBED = 64
        GP = 16
        PRE = [1, 2, 4]
        N_LEVELS = 3
        FUSED = EMBED * N_LEVELS

        def hilbert_flat_indices(n):
            t = np.arange(n * n, dtype=np.int64)
            x = np.zeros(n * n, dtype=np.int64)
            y = np.zeros(n * n, dtype=np.int64)
            s = 1
            while s < n:
                rx = 1 & t // 2
                ry = 1 & (t ^ rx)
                swap = ry == 0
                flip = swap & (rx == 1)
                x = np.where(flip, s - 1 - x, x)
                y = np.where(flip, s - 1 - y, y)
                x2 = np.where(swap, y, x)
                y2 = np.where(swap, x, y)
                x, y = (x2, y2)
                x = x + s * rx
                y = y + s * ry
                t = t // 4
                s *= 2
            return y * n + x

        def _level(x, idx, W, b, p, gp):
            Bsz, C, H, _ = x.shape
            h = H // p
            t = x.reshape(Bsz, C, h, p, h, p).transpose(0, 2, 4, 3, 5, 1).reshape(Bsz, h * h, p * p * C)
            t = t[:, idx]
            t = t.reshape(Bsz, h * h // gp, gp * p * p * C)
            return t @ W.T + b

        def _interp_linear(x, n_out):
            L = x.shape[1]
            pos = (jnp.arange(n_out, dtype=jnp.float32) + 0.5) * (L / n_out) - 0.5
            pos = jnp.clip(pos, 0.0, L - 1)
            i0 = jnp.floor(pos).astype(jnp.int32)
            i1 = jnp.minimum(i0 + 1, L - 1)
            w = (pos - i0).astype(x.dtype)
            return x[:, i0] * (1.0 - w)[None, :, None] + x[:, i1] * w[None, :, None]
        key = jax.random.key(seed)
        ks = jax.random.split(key, 9)
        inp = {'x': jax.random.normal(ks[0], (B, CH, IMG, IMG), jnp.float32)}
        for i, p in enumerate(PRE):
            din = CH * p * p * GP
            inp[f'W{i}'] = jax.random.normal(ks[1 + 2 * i], (EMBED, din), jnp.float32) * din ** (-0.5)
            inp[f'b{i}'] = jax.random.normal(ks[2 + 2 * i], (EMBED,), jnp.float32) * 0.02
        inp['Wf'] = jax.random.normal(ks[7], (FUSED, FUSED), jnp.float32) * FUSED ** (-0.5)
        inp['bf'] = jax.random.normal(ks[8], (FUSED,), jnp.float32) * 0.02
        for i, p in enumerate(PRE):
            inp[f'idx{i}'] = jnp.asarray(hilbert_flat_indices(IMG // p), jnp.int32)
        return inp
    _L0_tok_all = _L0_tok_setup()
    _L0_tok_in = {k: v for k, v in _L0_tok_all.items() if k in ('W0', 'b0', 'W1', 'b1', 'W2', 'b2', 'Wf', 'bf', 'idx0', 'idx1', 'idx2')}
    del _L0_tok_all

    def _L0_attn_setup():
        import jax, jax.numpy as jnp
        import numpy as np
        key = jax.random.key(seed)
        ks = jax.random.split(key, 4)
        B, S, D = (8, 512, 192)
        lim = (6.0 / (D + D)) ** 0.5
        Z = jax.random.normal(ks[0], (B, S, D), dtype=jnp.float32)
        Wq = jax.random.uniform(ks[1], (D, D), dtype=jnp.float32, minval=-lim, maxval=lim)
        Wk = jax.random.uniform(ks[2], (D, D), dtype=jnp.float32, minval=-lim, maxval=lim)
        Wv = jax.random.uniform(ks[3], (D, D), dtype=jnp.float32, minval=-lim, maxval=lim)
        bq = jnp.zeros((D,), dtype=jnp.float32)
        bk = jnp.zeros((D,), dtype=jnp.float32)
        bv = jnp.zeros((D,), dtype=jnp.float32)
        return {'Z': Z, 'Wq': Wq, 'bq': bq, 'Wk': Wk, 'bk': bk, 'Wv': Wv, 'bv': bv}
    _L0_attn_all = _L0_attn_setup()
    _L0_attn_in = {k: v for k, v in _L0_attn_all.items() if k in ('Wq', 'bq', 'Wk', 'bk', 'Wv', 'bv')}
    del _L0_attn_all

    def _L0_ffn_setup():
        import jax, jax.numpy as jnp
        import numpy as np
        E, C, F, K = (8, 192, 768, 2)
        key = jax.random.key(seed)
        k0, k1, k2, k3 = jax.random.split(key, 4)
        B, T = (8, 512)
        return {'x': jax.random.normal(k0, (B, T, C), jnp.float32), 'router_w': jax.random.normal(k1, (E, C), jnp.float32) * 0.02, 'w1': jax.random.normal(k2, (E, C, F), jnp.float32) * 0.02, 'b1': jnp.zeros((E, F), jnp.float32), 'w2': jax.random.normal(k3, (E, F, C), jnp.float32) * 0.02, 'b2': jnp.zeros((E, C), jnp.float32)}
    _L0_ffn_all = _L0_ffn_setup()
    _L0_ffn_in = {k: v for k, v in _L0_ffn_all.items() if k in ('router_w', 'w1', 'b1', 'w2', 'b2')}
    del _L0_ffn_all
    return {'x': x, 'L0_tok_W0': _L0_tok_in['W0'], 'L0_tok_b0': _L0_tok_in['b0'], 'L0_tok_W1': _L0_tok_in['W1'], 'L0_tok_b1': _L0_tok_in['b1'], 'L0_tok_W2': _L0_tok_in['W2'], 'L0_tok_b2': _L0_tok_in['b2'], 'L0_tok_Wf': _L0_tok_in['Wf'], 'L0_tok_bf': _L0_tok_in['bf'], 'L0_tok_idx0': _L0_tok_in['idx0'], 'L0_tok_idx1': _L0_tok_in['idx1'], 'L0_tok_idx2': _L0_tok_in['idx2'], 'L0_attn_Wq': _L0_attn_in['Wq'], 'L0_attn_bq': _L0_attn_in['bq'], 'L0_attn_Wk': _L0_attn_in['Wk'], 'L0_attn_bk': _L0_attn_in['bk'], 'L0_attn_Wv': _L0_attn_in['Wv'], 'L0_attn_bv': _L0_attn_in['bv'], 'L0_ffn_router_w': _L0_ffn_in['router_w'], 'L0_ffn_w1': _L0_ffn_in['w1'], 'L0_ffn_b1': _L0_ffn_in['b1'], 'L0_ffn_w2': _L0_ffn_in['w2'], 'L0_ffn_b2': _L0_ffn_in['b2']}

def reference(x, L0_tok_W0, L0_tok_b0, L0_tok_W1, L0_tok_b1, L0_tok_W2, L0_tok_b2, L0_tok_Wf, L0_tok_bf, L0_tok_idx0, L0_tok_idx1, L0_tok_idx2, L0_attn_Wq, L0_attn_bq, L0_attn_Wk, L0_attn_bk, L0_attn_Wv, L0_attn_bv, L0_ffn_router_w, L0_ffn_w1, L0_ffn_b1, L0_ffn_w2, L0_ffn_b2):
    import jax
    import jax.numpy as jnp

    def _L0_tok_ref(x, W0, b0, W1, b1, W2, b2, Wf, bf, idx0, idx1, idx2):
        import jax, jax.numpy as jnp
        import numpy as np
        B = 16
        IMG = 64
        CH = 3
        EMBED = 64
        GP = 16
        PRE = [1, 2, 4]
        N_LEVELS = 3
        FUSED = EMBED * N_LEVELS

        def hilbert_flat_indices(n):
            t = np.arange(n * n, dtype=np.int64)
            x = np.zeros(n * n, dtype=np.int64)
            y = np.zeros(n * n, dtype=np.int64)
            s = 1
            while s < n:
                rx = 1 & t // 2
                ry = 1 & (t ^ rx)
                swap = ry == 0
                flip = swap & (rx == 1)
                x = np.where(flip, s - 1 - x, x)
                y = np.where(flip, s - 1 - y, y)
                x2 = np.where(swap, y, x)
                y2 = np.where(swap, x, y)
                x, y = (x2, y2)
                x = x + s * rx
                y = y + s * ry
                t = t // 4
                s *= 2
            return y * n + x

        def _level(x, idx, W, b, p, gp):
            Bsz, C, H, _ = x.shape
            h = H // p
            t = x.reshape(Bsz, C, h, p, h, p).transpose(0, 2, 4, 3, 5, 1).reshape(Bsz, h * h, p * p * C)
            t = t[:, idx]
            t = t.reshape(Bsz, h * h // gp, gp * p * p * C)
            return t @ W.T + b

        def _interp_linear(x, n_out):
            L = x.shape[1]
            pos = (jnp.arange(n_out, dtype=jnp.float32) + 0.5) * (L / n_out) - 0.5
            pos = jnp.clip(pos, 0.0, L - 1)
            i0 = jnp.floor(pos).astype(jnp.int32)
            i1 = jnp.minimum(i0 + 1, L - 1)
            w = (pos - i0).astype(x.dtype)
            return x[:, i0] * (1.0 - w)[None, :, None] + x[:, i1] * w[None, :, None]
        Ws = [(idx0, W0, b0, PRE[0]), (idx1, W1, b1, PRE[1]), (idx2, W2, b2, PRE[2])]
        outs = [_level(x, idx, W, b, p, GP) for idx, W, b, p in Ws]
        n_tokens = outs[0].shape[1]
        outs = [outs[0]] + [_interp_linear(o, n_tokens) for o in outs[1:]]
        y = jnp.concatenate(outs, axis=-1)
        return y @ Wf.T + bf

    def _L0_attn_ref(Z, Wq, bq, Wk, bk, Wv, bv):
        import jax, jax.numpy as jnp
        import numpy as np
        D = Z.shape[-1]
        scale = 1.0 / D ** 0.5
        Q = jnp.einsum('bsd,ed->bse', Z, Wq) + bq
        K = jnp.einsum('bsd,ed->bse', Z, Wk) + bk
        V = jnp.einsum('bsd,ed->bse', Z, Wv) + bv
        scores = jnp.einsum('bqd,bkd->bqk', Q, K) * scale
        attn = jax.nn.softmax(scores, axis=-1)
        Z_hat = jnp.einsum('bqk,bkd->bqd', attn, V)
        return Z_hat

    def _L0_ffn_ref(x, router_w, w1, b1, w2, b2):
        import jax, jax.numpy as jnp
        import numpy as np
        E, C, F, K = (8, 192, 768, 2)
        B, T, Cc = x.shape
        flat = x.reshape(-1, Cc)
        logits = flat @ router_w.T
        probs = jax.nn.softmax(logits.astype(jnp.float32), axis=-1)
        top_w, top_i = jax.lax.top_k(probs, K)
        top_w = (top_w / top_w.sum(-1, keepdims=True)).astype(x.dtype)
        out = jnp.zeros_like(flat)
        for e in range(E):
            w_e = jnp.sum(top_w * (top_i == e), axis=-1)[:, None]
            h = jax.nn.gelu(flat @ w1[e] + b1[e], approximate=False)
            out = out + w_e * (h @ w2[e] + b2[e])
        return out.reshape(B, T, Cc)
    h = _L0_tok_ref(x, L0_tok_W0, L0_tok_b0, L0_tok_W1, L0_tok_b1, L0_tok_W2, L0_tok_b2, L0_tok_Wf, L0_tok_bf, L0_tok_idx0, L0_tok_idx1, L0_tok_idx2)
    h = h + _L0_attn_ref(_layernorm(h, axis=-1), L0_attn_Wq, L0_attn_bq, L0_attn_Wk, L0_attn_bk, L0_attn_Wv, L0_attn_bv)
    h = h + _L0_ffn_ref(_layernorm(h, axis=-1), L0_ffn_router_w, L0_ffn_w1, L0_ffn_b1, L0_ffn_w2, L0_ffn_b2)
    return h

_drawn_inputs = setup_inputs


def setup_inputs(seed=0):
    import zlib

    import numpy as np

    out = dict(_drawn_inputs(seed))
    spreads = {'L0_attn_bq': (0.0, 0.364),
     'L0_attn_bk': (0.0, 0.8),
     'L0_attn_bv': (0.0, 0.1),
     'L0_ffn_b1': (0.0, 0.349),
     'L0_ffn_b2': (0.0, 0.1)}
    factors = {}
    for name, (base, spread) in spreads.items():
        noise = np.random.default_rng([zlib.crc32(name.encode()), seed]).standard_normal(out[name].shape)
        drawn = base * np.exp(spread * noise) if base else spread * noise
        out[name] = jnp.asarray(drawn.astype(out[name].dtype))
    for name, factor in factors.items():
        out[name] = (out[name] * factor).astype(out[name].dtype)
    return out
```

```python
import numpy as np
import concourse.bass as bass
from concourse import mybir
from contextlib import ExitStack

BATCH, CHANNELS, IMAGE = 2, 3, 64
GROUP = 16
EMBED, LEVELS = 64, 3
MODEL = EMBED * LEVELS
EXPERTS, HIDDEN = 8, 768
SEQ = IMAGE * IMAGE // GROUP
TOKENS = BATCH * SEQ
PATCHES = [4096, 1024, 256]
LEVEL_TOKENS = [n // GROUP for n in PATCHES]
FEATURES = [3, 12, 48]
P = 128
LOW = 256
GATHER_ROWS = 48
B1 = 64
ROWS = B1 + GATHER_ROWS
PICKS = sum(PATCHES)
START = [PATCHES[1] + PATCHES[2], PATCHES[2], 0]
TOKEN_TILES = TOKENS // P
C0, C1 = P, MODEL - P
SLOT_TILES = 2 * TOKENS // P + EXPERTS - 1
AHEAD = 3
TABLE = 2 * ((SLOT_TILES + AHEAD) // 2 + 1)
FK = HIDDEN // P
NH = HIDDEN // 2
EPS = 1e-5

K_IDENT = 0
K_TRI = K_IDENT + P
K_IOTA = K_TRI + P
K_UP1 = K_IOTA + P
K_UP2 = K_UP1 + SEQ
K_LOW = K_UP2 + SEQ
K_HIGH = K_LOW + 2
K_TOKEN = K_HIGH + LEVELS
K_HALF = K_TOKEN + TOKEN_TILES
K_END = K_HALF + TOKEN_TILES


def build(nc, xt, idx, we, embed_bias, wf, bf, wq, wk, wv, router, w1, b1, w2, b2, consts, out):
    F, R, I32, U32, U8, BF = (mybir.dt.float32, mybir.dt.float32r, mybir.dt.int32, mybir.dt.uint32,
                              mybir.dt.uint8, mybir.dt.bfloat16)
    ALU, ACT, AX = mybir.AluOpType, mybir.ActivationFunctionType, mybir.AxisListType
    ctx = ExitStack()
    with ctx:
        def sb(name, shape, dt=F):
            return ctx.enter_context(nc.sbuf_tensor(name, shape, dt))

        def sem(name):
            return ctx.enter_context(nc.semaphore(name))

        z2_dram = nc.dram_tensor("z2_dram", (TOKENS, MODEL), F).ap()

        K = sb("K", [P, K_END])
        ident, tri, iota = K[:, K_IDENT:K_TRI], K[:, K_TRI:K_IOTA], K[:, K_IOTA:K_UP1]
        xtab = sb("xtab", [P, 2 * LEVELS, ROWS])
        xtab_hi = sb("xtab_hi", [P, 2 * LEVELS, ROWS], R)
        xtab_lo = sb("xtab_lo", [P, 2 * LEVELS, ROWS], R)
        picks = sb("picks", [P, PICKS], I32)
        pick_bytes = picks[:, :].bitcast(U8).rearrange("p (j f) -> p j f", f=4)
        onehot = sb("onehot", [P, 2, 2, 512], R)
        gathered = sb("gathered", [P, PICKS])
        old_picks, old_gathered = picks[:, :].bitcast(F), gathered[:, :]

        def cut(space, start, *dims):
            view = space[:, start:start + int(np.prod(dims))]
            names = " ".join("abc"[:len(dims)])
            return view.rearrange(f"p ({names}) -> p {names}", **dict(zip("abc", dims))) if len(dims) > 1 else view

        probs = cut(old_picks, 0, TOKEN_TILES, SEQ)
        probs_t = cut(old_picks, 1024, TOKEN_TILES, 2, P)
        qt0 = cut(old_picks, 2048, TOKENS)
        qt1 = cut(old_picks, 2560, TOKENS)[0:C1 + 1]
        v_sb = cut(old_picks, 3072, TOKEN_TILES, MODEL)
        out_init = cut(old_picks, 3840, TOKEN_TILES, MODEL)
        z2t0 = cut(old_gathered, 0, TOKENS)
        z2t1 = cut(old_gathered, 512, TOKENS)[0:C1]
        z2 = cut(old_gathered, 1024, TOKEN_TILES, MODEL)
        in_row = onehot[:, :, :, :].rearrange("p a b (c r) -> p (a b c) r", r=P)[:, 0:2 * TOKEN_TILES, :]
        we_sb = sb("we_sb", [P, LEVELS, GROUP, EMBED])
        ebias = sb("ebias", [P, LEVELS])
        t12 = sb("t12", [B1, 2, P])
        cat = sb("cat", [P, LEVELS, SEQ])
        wf_sb = sb("wf_sb", [P, LEVELS, MODEL])
        bf_sb = sb("bf_sb", [P, MODEL])
        wq0, wq1 = sb("wq0", [C0, MODEL + 1]), sb("wq1", [C1, MODEL + 1])
        wk0, wk1 = sb("wk0", [C0, MODEL + 1]), sb("wk1", [C1, MODEL + 1])
        wv0, wv1 = sb("wv0", [C0, MODEL]), sb("wv1", [C1 + 1, MODEL])
        qk0, qk1 = sb("qk0", [C0, MODEL + 1]), sb("qk1", [C1 + 1, MODEL + 1])
        h = sb("h", [P, TOKEN_TILES, MODEL])
        stats = sb("stats", [P, TOKEN_TILES, 6])
        mv = sb("mv", [P, TOKEN_TILES, 2])
        vareps = sb("vareps", [P, TOKEN_TILES])
        rstd = sb("rstd", [P, TOKEN_TILES])
        z = sb("z", [P, TOKEN_TILES, MODEL])
        zt0, zt1 = sb("zt0", [C0, TOKENS]), sb("zt1", [C1 + 1, TOKENS])
        nmax = sb("nmax", [P, TOKEN_TILES])
        esum = sb("esum", [P, TOKEN_TILES])
        rsum = sb("rsum", [P, TOKEN_TILES])
        h2 = sb("h2", [P, TOKEN_TILES, MODEL])
        rw0, rw1 = sb("rw0", [C0, EXPERTS]), sb("rw1", [C1, EXPERTS])
        b2_sb = sb("b2_sb", [EXPERTS, MODEL])
        ones_b = sb("ones_b", [P, P], BF)
        tri_b = sb("tri_b", [P, P], BF)
        ones8 = sb("ones8", [P, EXPERTS])
        logits = sb("logits", [P, TOKEN_TILES, EXPERTS])
        top = sb("top", [P, TOKEN_TILES, EXPERTS])
        topi = sb("topi", [P, TOKEN_TILES, EXPERTS], U32)
        topf = sb("topf", [P, 2, TOKEN_TILES])
        gap = sb("gap", [P, TOKEN_TILES])
        egap = sb("egap", [P, TOKEN_TILES])
        eden = sb("eden", [P, TOKEN_TILES])
        wgt = sb("wgt", [P, 2, TOKEN_TILES])
        chosen = sb("chosen", [P, 2, TOKEN_TILES, EXPERTS])
        member = sb("member", [P, TOKEN_TILES, EXPERTS], BF)
        cntf = sb("cntf", [P, EXPERTS])
        cnti = sb("cnti", [P, EXPERTS], I32)
        cntt = sb("cntt", [P, EXPERTS], I32)
        ntile = sb("ntile", [P, EXPERTS])
        tile_end = sb("tile_end", [P, EXPERTS])
        base = sb("base", [P, EXPERTS])
        slot = sb("slot", [P, TOKEN_TILES, EXPERTS])
        picked = sb("picked", [P, 2, TOKEN_TILES, EXPERTS])
        slotf = sb("slotf", [P, 2 * TOKEN_TILES])
        sloti = sb("sloti", [P, 2 * TOKEN_TILES], I32)
        slot_tile_i = sb("slot_tile_i", [P, 2 * TOKEN_TILES], I32)
        slot_row_i = sb("slot_row_i", [P, 2 * TOKEN_TILES], I32)
        slot_tile = sb("slot_tile", [P, 2 * TOKEN_TILES])
        slot_row = sb("slot_row", [P, 2 * TOKEN_TILES])
        in_tile = sb("in_tile", [P, 2 * TOKEN_TILES, TABLE])
        payload = sb("payload", [P, 2 * TOKEN_TILES, 3, TABLE], R)
        wpart = sb("wpart", [P, 2 * TOKEN_TILES, TABLE])
        table = sb("table", [P, 3, TABLE])
        slot_w = sb("slot_w", [P, TABLE])
        gidx = sb("gidx", [P, TABLE], I32)
        pad = sb("pad", [P, TABLE])
        sidxf = sb("sidxf", [P, TABLE])
        sidx = sb("sidx", [P, TABLE], I32)
        before = sb("before", [P, TABLE, EXPERTS])
        expertf = sb("expertf", [P, TABLE])
        expert = sb("expert", [P, TABLE], I32)
        tiles_used = sb("tiles_used", [P, 1], I32)
        comb = sb("comb", [P, TOKEN_TILES, EXPERTS])
        comb2 = sb("comb2", [P, TOKEN_TILES, EXPERTS])
        comb_t = sb("comb_t", [EXPERTS, TOKENS])
        w1_0 = sb("w1_0", [C0, EXPERTS * HIDDEN])
        w1_1 = sb("w1_1", [C1 + 1, EXPERTS * HIDDEN])
        w2_sb = sb("w2_sb", [P, EXPERTS * FK * MODEL])
        gi_col = [sb(f"gi_col{i}", [P, 1], I32) for i in range(2)]
        si_col = [sb(f"si_col{i}", [P, 1], I32) for i in range(2)]
        xg = [sb(f"xg{i}", [P, MODEL]) for i in range(2)]
        xs0 = [sb(f"xs0_{i}", [C0, P]) for i in range(2)]
        xs1 = [sb(f"xs1_{i}", [C1 + 1, P]) for i in range(2)]
        hid = sb("hid", [P, HIDDEN])
        hid_t = sb("hid_t", [P, FK, P])
        ys = [sb(f"ys{i}", [P, MODEL]) for i in range(2)]

        bank = [ctx.enter_context(nc.psum_tensor(f"bank{i}", [P, 512], F)) for i in range(8)]

        k_in, x_in, we_in, wf_in = sem("k_in"), sem("x_in"), sem("we_in"), sem("wf_in")
        attn_in, misc_in, moe_in = sem("attn_in"), sem("misc_in"), sem("moe_in")
        pick_in = [sem(f"pick_in{i}") for i in range(4)]
        dv, gp_set = sem("dv"), sem("gp_set")
        xtab_ready, onehot_ready, picked_psum, picked_sb = (sem("xtab_ready"), sem("onehot_ready"),
                                                            sem("picked_psum"), sem("picked_sb"))
        tok_psum, tok_sb, cat_psum, cat_sb = sem("tok_psum"), sem("tok_sb"), sem("cat_psum"), sem("cat_sb")
        qk_psum, qk_sb = sem("qk_psum"), sem("qk_sb")
        h_psum, h_ready, var_ready, rstd_ready = sem("h_psum"), sem("h_ready"), sem("var_ready"), sem("rstd_ready")
        z_ready, zt_psum, zt_sb = sem("z_ready"), sem("zt_psum"), sem("zt_sb")
        v_psum, v_ready, q_psum, q_sb = sem("v_psum"), sem("v_ready"), sem("q_psum"), sem("q_sb")
        score_psum, nmax_ready, probs_ready = sem("score_psum"), sem("nmax_ready"), sem("probs_ready")
        pt_psum, pt_sb, pv_psum = sem("pt_psum"), sem("pt_sb"), sem("pv_psum")
        var2_ready, rstd2_ready, z2_ready = sem("var2_ready"), sem("rstd2_ready"), sem("z2_ready")
        z2_stored, z2t_psum, z2t_sb, logit_psum = sem("z2_stored"), sem("z2t_psum"), sem("z2t_sb"), sem("logit_psum")
        gap_ready, egap_ready, member_ready, rank_psum = (sem("gap_ready"), sem("egap_ready"),
                                                          sem("member_ready"), sem("rank_psum"))
        payload_ready, table_psum, table_ready = sem("payload_ready"), sem("table_psum"), sem("table_ready")
        comb_ready, comb_psum, comb_sb, init_psum, init_sb = (sem("comb_ready"), sem("comb_psum"), sem("comb_sb"),
                                                              sem("init_psum"), sem("init_sb"))
        out_stored = sem("out_stored")
        column_ready, gather_done, xt_psum, xt_copied = (sem("column_ready"), sem("gather_done"),
                                                         sem("xt_psum"), sem("xt_copied"))
        up_psum, gelu_done, ht_psum, ht_act, ht_dve = (sem("up_psum"), sem("gelu_done"), sem("ht_psum"),
                                                       sem("ht_act"), sem("ht_dve"))
        y_psum, y_free, ys_free, y_ready, scatter_done, pool_mark = (sem("y_psum"), sem("y_free"), sem("ys_free"), sem("y_ready"),
                                                            sem("scatter_done"), sem("pool_mark"))

        pieces = [(2, START[2], PATCHES[2], 0)]
        pieces += [(1, START[1] + 512 * i, 512, 1) for i in range(PATCHES[1] // 512)]
        pieces += [(0, START[0] + 512 * i, 512, 2 + i // 4) for i in range(PATCHES[0] // 512)]
        piece_span = [(0, START[1]), (START[1], START[0]), (START[0], START[0] + 2048), (START[0] + 2048, PICKS)]

        def tokens(b, half):
            return (2 * b + half) * P

        block = ctx.enter_context(nc.Block())

        @block.sync
        def _(sp):
            sp.dma_start(K[:, :], consts).then_inc(k_in, 16)
            xin = xt.rearrange("p t (b r) -> p t b r", b=2)
            for b in range(BATCH):
                sp.dma_start(xtab[:, :, B1 * b:B1 * b + GATHER_ROWS], xin[:, :, b, :]).then_inc(x_in, 16)
            for n, (lo, hi) in enumerate(piece_span):
                sp.dma_start(picks[:, lo:hi], idx[lo:hi].partition_broadcast(P)).then_inc(pick_in[n], 16)
            for e in range(EXPERTS):
                w1e = w1[e, :, :]
                sp.dma_start(w1_0[:, e * HIDDEN:(e + 1) * HIDDEN], w1e[0:C0, :]).then_inc(moe_in, 16)
                sp.dma_start(w1_1[0:C1, e * HIDDEN:(e + 1) * HIDDEN], w1e[C0:MODEL, :]).then_inc(moe_in, 16)
                sp.dma_start(w2_sb[:, e * FK * MODEL:(e + 1) * FK * MODEL].rearrange("p (k c) -> p k c", k=FK),
                             w2[e, :, :].rearrange("(k p) c -> p k c", p=P)).then_inc(moe_in, 16)
            sp.dma_start(w1_1[C1:C1 + 1, :], b1).then_inc(moe_in, 16)
            for t in range(TOKEN_TILES):
                sp.wait_ge(z2_ready, t + 1)
                sp.dma_start(z2_dram[t * P:(t + 1) * P, :], z2[:, t, :]).then_inc(z2_stored, 16)
            for b in range(BATCH):
                sp.wait_ge(init_sb, b + 1)
                sp.dma_start(out.rearrange("(t p) c -> p t c", p=P)[:, 2 * b:2 * b + 2, :],
                             out_init[:, 2 * b:2 * b + 2, :]).then_inc(out_stored, 16)
            sp.wait_ge(out_stored, 16 * BATCH)

        @block.gpsimd
        def _(pool):
            pool.wait_ge(k_in, 16)
            nc.gpsimd.tensor_copy(tri_b[:, :], tri).then_inc(gp_set, 1)
            half = K[:, K_HALF:K_HALF + TOKEN_TILES]
            pool.wait_ge(var_ready, 1)
            nc.gpsimd.tensor_tensor(rstd[:, :], vareps[:, :], half, ALU.pow).then_inc(rstd_ready, 1)
            pool.wait_ge(var2_ready, 1)
            nc.gpsimd.tensor_tensor(rstd[:, :], vareps[:, :], half, ALU.pow).then_inc(rstd2_ready, 1)

            def gather(j, par):
                nc.gpsimd.tensor_copy(gi_col[par][:, :], gidx[:, bass.ds(j, 1)]).then_inc(column_ready, 1)

            def gather_start(par):
                nc.gpsimd.indirect_dma_start(
                    out=xg[par][:, :], out_offset=None, in_=z2_dram,
                    in_offset=bass.IndirectOffsetOnAxis(gi_col[par][:, 0:1].bitcast(U32), 0)).then_inc(gather_done, 16)

            pool.wait_ge(table_ready, 1)
            pool.wait_ge(z2_stored, 16 * TOKEN_TILES)
            for j in range(AHEAD):
                if j >= 1:
                    pool.wait_ge(gather_done, 16 * j)
                if j >= 2:
                    pool.wait_ge(xt_psum, j - 1)
                gather(j, j % 2)
                pool.wait_ge(column_ready, j + 1)
                gather_start(j % 2)
            pool.sem_inc(ys_free, 2)
            pool.wait_ge(out_stored, 16 * BATCH)
            used = pool.value_load(tiles_used[0:1, 0:1], min_val=1, max_val=SLOT_TILES)
            with pool.Fori(0, (SLOT_TILES + 1) // 2) as i:
                for par in range(2):
                    with pool.If(2 * i + par < used):
                        j = 2 * i + par
                        pool.wait_ge(xt_psum, j + 2)
                        pool.sem_inc(pool_mark, 1)
                        pool.wait_ge(gather_done, 16 * j + 16 * AHEAD)
                        pool.sem_inc(pool_mark, 1)
                        gather(j + AHEAD, (par + 1) % 2)
                        pool.wait_ge(column_ready, 2 * j + AHEAD + 1)
                        pool.sem_inc(pool_mark, 1)
                        gather_start((par + 1) % 2)
                        nc.gpsimd.tensor_copy(si_col[par][:, :], sidx[:, bass.ds(j, 1)]).then_inc(column_ready, 1)
                        pool.wait_ge(column_ready, 2 * j + AHEAD + 2)
                        pool.sem_inc(pool_mark, 1)
                        pool.wait_ge(y_ready, j + 1)
                        pool.sem_inc(pool_mark, 1)
                        nc.gpsimd.indirect_dma_start(
                            out=out, out_offset=bass.IndirectOffsetOnAxis(si_col[par][:, 0:1].bitcast(U32), 0),
                            in_=ys[par][:, :], in_offset=None, bounds_check=TOKENS - 1, oob_is_err=False,
                            compute_op=ALU.add).then_inc(scatter_done, 16)
                        pool.wait_ge(scatter_done, 16 * j + 16)
                        pool.sem_inc(ys_free, 1)
            pool.wait_ge(gather_done, used * 16 + 16 * AHEAD)
            pool.sem_inc(pool_mark, 1)

        @block.scalar
        def _(act):
            for level in (2, 1, 0):
                highs, f = GATHER_ROWS // FEATURES[level], FEATURES[level]
                for b in range(BATCH):
                    for g in range(highs):
                        r = B1 * b + g * f
                        act.dma_start(we_sb[r:r + f, level, :, :], we[level]).then_inc(we_in, 16)
            for b in range(BATCH):
                act.dma_start(ebias[B1 * b:B1 * b + EMBED, :], embed_bias).then_inc(wf_in, 16)
                act.dma_start(wf_sb[B1 * b:B1 * b + EMBED, :, :], wf).then_inc(wf_in, 16)
            act.dma_start(bf_sb[:, :], bf.partition_broadcast(P)).then_inc(wf_in, 16)
            for dst, src, rows in ((wq0, wq, (0, C0)), (wq1, wq, (C0, MODEL)), (wk0, wk, (0, C0)),
                                   (wk1, wk, (C0, MODEL)), (wv0, wv, (0, C0)), (wv1, wv, (C0, MODEL + 1))):
                act.dma_start(dst[:, :], src[rows[0]:rows[1], :]).then_inc(attn_in, 16)
            act.dma_start(rw0[:, :], router[0:C0, :]).then_inc(misc_in, 16)
            act.dma_start(rw1[:, :], router[C0:MODEL, :]).then_inc(misc_in, 16)
            act.dma_start(b2_sb[:, :], b2).then_inc(misc_in, 16)
            act.wait_ge(qk_psum, 1)
            nc.scalar.mul(qk0[:, :], bank[6][0:C0, 256:257 + MODEL], float(MODEL) ** -0.5).then_inc(qk_sb, 1)
            nc.scalar.mul(qk1[:, :], bank[7][0:C1 + 1, 256:257 + MODEL], float(MODEL) ** -0.5).then_inc(qk_sb, 1)
            for n, (rows, col, k) in enumerate(((LEVEL_TOKENS[2], EMBED, 1), (LEVEL_TOKENS[1], 0, 0))):
                act.wait_ge(tok_psum, n + 1)
                for b in range(BATCH):
                    nc.scalar.copy(t12[0:rows, k, EMBED * b:EMBED * (b + 1)],
                                   bank[2 + b][0:rows, col:col + EMBED]).then_inc(tok_sb, 1)
            act.wait_ge(wf_in, 16 * 5)
            for level in (2, 1):
                act.wait_ge(cat_psum, 3 - level)
                nc.scalar.activation(cat[:, level, :], bank[5 + level][:, 0:SEQ], ACT.Identity,
                                     bias=ebias[:, level:level + 1]).then_inc(cat_sb, 1)
            act.wait_ge(cat_psum, 3)
            for b in range(BATCH):
                r = slice(B1 * b, B1 * b + EMBED)
                nc.scalar.activation(cat[r, 0, :], bank[4 + b][r, 0:SEQ], ACT.Identity,
                                     bias=ebias[r, 0:1]).then_inc(cat_sb, 1)
            act.wait_ge(zt_psum, 1)
            nc.scalar.copy(zt0[:, 0:SEQ], bank[2][:, 0:SEQ])
            nc.scalar.copy(zt1[0:C1, 0:SEQ], bank[2][0:C1, SEQ:2 * SEQ]).then_inc(zt_sb, 1)
            act.wait_ge(q_psum, 1)
            nc.scalar.copy(qt0[:, :], bank[6][:, :]).then_inc(q_sb, 1)
            act.wait_ge(v_psum, 1)
            nc.scalar.copy(v_sb[:, 0:2, :], bank[4][:, 0:2 * MODEL]).then_inc(v_ready, 1)
            for t in range(TOKEN_TILES):
                act.wait_ge(nmax_ready, t // 2 + 1)
                nc.scalar.activation(probs[:, t, :], bank[t // 2][:, SEQ * (t % 2):SEQ * (t % 2 + 1)], ACT.Exp,
                                     bias=nmax[:, t:t + 1], accum_out=esum[:, t:t + 1]).then_inc(probs_ready, 1)
            act.wait_ge(pt_psum, 2)
            nc.scalar.copy(probs_t[:, 2:4, :, :], bank[3][:, :]).then_inc(pt_sb, 1)
            act.wait_ge(z2t_psum, 1)
            nc.scalar.copy(z2t0[:, 0:SEQ], bank[6][:, 0:SEQ])
            nc.scalar.copy(z2t1[:, 0:SEQ], bank[6][0:C1, SEQ:2 * SEQ]).then_inc(z2t_sb, 1)
            act.wait_ge(gap_ready, 1)
            nc.scalar.activation(egap[:, :], gap[:, :], ACT.Exp).then_inc(egap_ready, 1)
            act.wait_ge(comb_psum, 1)
            nc.scalar.copy(comb_t[:, :], bank[1][0:EXPERTS, :]).then_inc(comb_sb, 1)

            def gelu(par):
                for n in range(2):
                    last = nc.scalar.activation(hid[:, n * NH:(n + 1) * NH], bank[2 * par + n][:, 0:NH], ACT.Gelu)
                last.then_inc(gelu_done, 1)

            act.wait_ge(up_psum, 1)
            gelu(0)
            act.wait_ge(table_ready, 1)
            used = act.value_load(tiles_used[0:1, 0:1], min_val=1, max_val=SLOT_TILES)
            with act.Fori(0, (SLOT_TILES + 1) // 2) as i:
                for par in range(2):
                    with act.If(2 * i + par < used):
                        j = 2 * i + par
                        act.wait_ge(ht_psum, j + 1)
                        nc.scalar.copy(hid_t[:, 0:FK // 2, :], bank[4][:, 0:NH]).then_inc(ht_act, 1)
                        act.wait_ge(up_psum, j + 2)
                        gelu((par + 1) % 2)

        @block.vector
        def _(dve):
            chain = [0]

            def link(ins):
                chain[0] += 1
                ins.then_inc(dv, 1)
                dve.wait_ge(dv, chain[0])

            nc.vector.memset(zt1[C1:C1 + 1, :], 1.0).then_inc(gp_set, 1)
            nc.vector.memset(xs1[0][C1:C1 + 1, :], 1.0).then_inc(gp_set, 1)
            nc.vector.memset(xs1[1][C1:C1 + 1, :], 1.0).then_inc(gp_set, 1)
            nc.vector.memset(ones_b[:, :], 1.0).then_inc(gp_set, 1)
            nc.vector.memset(ones8[:, :], 1.0).then_inc(gp_set, 1)
            link(nc.vector.memset(xtab[:, :, GATHER_ROWS:B1], 0.0))
            dve.wait_ge(x_in, 32)
            link(nc.vector.tensor_copy(xtab_hi[:, :, :], xtab[:, :, :]))
            nc.vector.tensor_tensor(xtab_lo[:, :, :], xtab[:, :, :], xtab_hi[:, :, :].bitcast(F),
                                    ALU.subtract).then_inc(xtab_ready, 1)
            dve.wait_ge(k_in, 16)

            def make_onehot(n):
                level, col, width, piece = pieces[n]
                dve.wait_ge(pick_in[piece], 16)
                if n >= 2:
                    dve.wait_ge(picked_psum, n - 1)
                for k in range(2):
                    nc.vector.tensor_scalar(onehot[:, n % 2, k, 0:width], pick_bytes[:, col:col + width, 0],
                                            K[:, K_LOW + k:K_LOW + k + 1], None,
                                            ALU.is_equal).then_inc(onehot_ready, 1)

            def mask_high(n):
                level, col, width, piece = pieces[n]
                dve.wait_ge(picked_psum, n + 1)
                nc.vector.scalar_tensor_tensor(
                    out=gathered[0:ROWS, col:col + width], in0=pick_bytes[0:ROWS, col:col + width, 1],
                    scalar=K[0:ROWS, K_HIGH + level:K_HIGH + level + 1], in1=bank[n % 2][0:ROWS, 0:width],
                    op0=ALU.is_equal, op1=ALU.mult).then_inc(picked_sb, 1)

            make_onehot(0)
            for n in range(1, len(pieces)):
                make_onehot(n)
                mask_high(n - 1)
            mask_high(len(pieces) - 1)

            def layer_norm(src, ready, rstd_done, dst, done):
                for t in range(TOKEN_TILES):
                    last = nc.vector.bn_stats(stats[:, t, :], src[:, t, :])
                link(last)
                for t in range(TOKEN_TILES):
                    last = nc.vector.bn_aggr(mv[:, t, :], stats[:, t, :])
                link(last)
                nc.vector.tensor_scalar(vareps[:, :], mv[:, :, 1], EPS, None, ALU.add).then_inc(ready, 1)
                dve.wait_ge(rstd_done, 1)
                for t in range(TOKEN_TILES):
                    nc.vector.tensor_scalar(dst[:, t, :], src[:, t, :], mv[:, t, 0:1], rstd[:, t:t + 1],
                                            ALU.subtract, ALU.mult).then_inc(done, 1)

            dve.wait_ge(wf_in, 16 * 5)
            for b in range(BATCH):
                dve.wait_ge(h_psum, b + 1)
                last = nc.vector.tensor_tensor(
                    h[:, 2 * b:2 * b + 2, :], bank[b][:, 0:2 * MODEL].rearrange("p (t c) -> p t c", t=2),
                    bf_sb[:, None, :].to_broadcast([P, 2, MODEL]), ALU.add)
            link(last)
            layer_norm(h, var_ready, rstd_ready, z, z_ready)
            dve.wait_ge(gp_set, 6)
            dve.wait_ge(zt_psum, 2)
            nc.vector.tensor_copy(zt0[:, SEQ:2 * SEQ], bank[3][:, 0:SEQ])
            nc.vector.tensor_copy(zt1[0:C1, SEQ:2 * SEQ], bank[3][0:C1, SEQ:2 * SEQ]).then_inc(zt_sb, 1)
            dve.wait_ge(q_psum, 2)
            nc.vector.tensor_copy(qt1[:, :], bank[7][0:C1 + 1, :]).then_inc(q_sb, 1)
            dve.wait_ge(v_psum, 2)
            nc.vector.tensor_copy(v_sb[:, 2:4, :], bank[5][:, 0:2 * MODEL]).then_inc(v_ready, 1)
            for b in range(BATCH):
                dve.wait_ge(score_psum, b + 1)
                nc.vector.tensor_reduce(nmax[:, 2 * b:2 * b + 2],
                                        bank[b][:, :].rearrange("p (t k) -> p t k", t=2),
                                        AX.X, ALU.max, negate=True).then_inc(nmax_ready, 1)
            dve.wait_ge(pt_psum, 1)
            nc.vector.tensor_copy(probs_t[:, 0:2, :, :], bank[2][:, :]).then_inc(pt_sb, 1)
            dve.wait_ge(probs_ready, TOKEN_TILES)
            link(nc.vector.reciprocal(rsum[:, :], esum[:, :]))
            for t in range(TOKEN_TILES):
                dve.wait_ge(pv_psum, t // 2 + 1)
                last = nc.vector.scalar_tensor_tensor(
                    out=h2[:, t, :], in0=bank[4 + t // 2][:, MODEL * (t % 2):MODEL * (t % 2 + 1)],
                    scalar=rsum[:, t:t + 1], in1=h[:, t, :], op0=ALU.mult, op1=ALU.add)
            link(last)
            layer_norm(h2, var2_ready, rstd2_ready, z2, z2_ready)
            dve.wait_ge(z2t_psum, 2)
            nc.vector.tensor_copy(z2t0[:, SEQ:2 * SEQ], bank[7][:, 0:SEQ])
            nc.vector.tensor_copy(z2t1[:, SEQ:2 * SEQ], bank[7][0:C1, SEQ:2 * SEQ]).then_inc(z2t_sb, 1)

            dve.wait_ge(logit_psum, 1)
            link(nc.vector.tensor_copy(logits[:, :, :], bank[0][:, 0:TOKEN_TILES * EXPERTS]))
            for t in range(TOKEN_TILES):
                last = nc.vector.max(top[:, t, :], logits[:, t, :])
            link(last)
            nc.vector.tensor_tensor(gap[:, :], top[:, :, 1], top[:, :, 0], ALU.subtract).then_inc(gap_ready, 1)
            for t in range(TOKEN_TILES):
                last = nc.vector.max_index(topi[:, t, :], top[:, t, :], logits[:, t, :])
            link(last)
            link(nc.vector.tensor_copy(topf[:, :, :], topi[:, :, 0:2].rearrange("p t c -> p c t")))
            for c in range(2):
                last = nc.vector.tensor_tensor(
                    chosen[:, c, :, :], iota[:, None, 0:EXPERTS].to_broadcast([P, TOKEN_TILES, EXPERTS]),
                    topf[:, c, :, None].to_broadcast([P, TOKEN_TILES, EXPERTS]), ALU.is_equal)
            link(last)
            nc.vector.tensor_tensor(member[:, :, :], chosen[:, 0, :, :], chosen[:, 1, :, :],
                                    ALU.add).then_inc(member_ready, 1)
            dve.wait_ge(egap_ready, 1)
            link(nc.vector.tensor_scalar(eden[:, :], egap[:, :], 1.0, None, ALU.add))
            link(nc.vector.reciprocal(wgt[:, 0, :], eden[:, :]))
            link(nc.vector.tensor_tensor(wgt[:, 1, :], egap[:, :], wgt[:, 0, :], ALU.mult))
            for c, dst in ((0, comb), (1, comb2)):
                last = nc.vector.tensor_tensor(dst[:, :, :], chosen[:, c, :, :],
                                               wgt[:, c, :, None].to_broadcast([P, TOKEN_TILES, EXPERTS]), ALU.mult)
            link(last)
            nc.vector.tensor_tensor(comb[:, :, :], comb[:, :, :], comb2[:, :, :], ALU.add).then_inc(comb_ready, 1)
            dve.wait_ge(rank_psum, 1)
            link(nc.vector.tensor_scalar(cntf[:, :], bank[4][:, 32:32 + EXPERTS], float(P - 1), None, ALU.add))
            link(nc.vector.tensor_copy(cnti[:, :], cntf[:, :]))
            link(nc.vector.tensor_single_scalar(cntt[:, :], cnti[:, :], 7, ALU.logical_shift_right))
            link(nc.vector.tensor_copy(ntile[:, :], cntt[:, :]))
            link(nc.vector.tensor_tensor_scan(tile_end[:, :], ones8[:, :], ntile[:, :], 0.0, ALU.mult, ALU.add))
            link(nc.vector.tensor_tensor(base[:, :], tile_end[:, :], ntile[:, :], ALU.subtract))
            link(nc.vector.scalar_tensor_tensor(
                out=slot[:, :, :], in0=base[:, None, :].to_broadcast([P, TOKEN_TILES, EXPERTS]), scalar=float(P),
                in1=bank[4][:, 0:32].rearrange("p (t e) -> p t e", t=TOKEN_TILES), op0=ALU.mult, op1=ALU.add))
            link(nc.vector.tensor_tensor(picked[:, :, :, :], chosen[:, :, :, :],
                                         slot[:, None, :, :].to_broadcast([P, 2, TOKEN_TILES, EXPERTS]), ALU.mult))
            link(nc.vector.tensor_reduce(slotf[:, :], picked[:, :, :, :].rearrange("p c t e -> p (c t) e"),
                                         AX.X, ALU.add))
            link(nc.vector.tensor_copy(sloti[:, :], slotf[:, :]))
            nc.vector.tensor_single_scalar(slot_tile_i[:, :], sloti[:, :], 7, ALU.logical_shift_right)
            link(nc.vector.tensor_single_scalar(slot_row_i[:, :], sloti[:, :], P - 1, ALU.bitwise_and))
            nc.vector.tensor_copy(slot_tile[:, :], slot_tile_i[:, :])
            link(nc.vector.tensor_copy(slot_row[:, :], slot_row_i[:, :]))
            nc.vector.tensor_tensor(in_row[:, :, :], iota[:, None, :].to_broadcast([P, 8, P]),
                                    slot_row[:, :, None].to_broadcast([P, 8, P]), ALU.is_equal)
            link(nc.vector.tensor_tensor(in_tile[:, :, :], iota[:, None, 0:TABLE].to_broadcast([P, 8, TABLE]),
                                         slot_tile[:, :, None].to_broadcast([P, 8, TABLE]), ALU.is_equal))
            for c in range(2):
                nc.vector.tensor_tensor(
                    payload[:, 4 * c:4 * c + 4, 0, :], in_tile[:, 4 * c:4 * c + 4, :],
                    K[:, K_TOKEN:K_TOKEN + TOKEN_TILES, None].to_broadcast([P, TOKEN_TILES, TABLE]), ALU.mult)
            link(nc.vector.tensor_tensor(
                wpart[:, :, :], in_tile[:, :, :],
                wgt[:, :, :].rearrange("p c t -> p (c t)")[:, :, None].to_broadcast([P, 8, TABLE]), ALU.mult))
            link(nc.vector.tensor_copy(payload[:, :, 1, :], wpart[:, :, :]))
            nc.vector.tensor_tensor(payload[:, :, 2, :], wpart[:, :, :], payload[:, :, 1, :].bitcast(F),
                                    ALU.subtract).then_inc(payload_ready, 1)
            link(nc.vector.tensor_tensor(before[:, :, :], tile_end[:, None, :].to_broadcast([P, TABLE, EXPERTS]),
                                         iota[:, 0:TABLE, None].to_broadcast([P, TABLE, EXPERTS]), ALU.is_le))
            link(nc.vector.tensor_reduce(expertf[:, :], before[:, :, :], AX.X, ALU.add))
            nc.vector.tensor_scalar(expert[:, :], expertf[:, :], float(EXPERTS - 1), None, ALU.min)
            link(nc.vector.tensor_copy(tiles_used[:, :], tile_end[:, EXPERTS - 1:EXPERTS]))
            dve.wait_ge(table_psum, 1)
            link(nc.vector.tensor_copy(table[:, :, :], bank[5][:, 0:3 * TABLE]))
            nc.vector.tensor_tensor(slot_w[:, :], table[:, 1, :], table[:, 2, :], ALU.add)
            nc.vector.tensor_scalar(gidx[:, :], table[:, 0, :], 1.0, 0.0, ALU.subtract, ALU.max)
            link(nc.vector.tensor_scalar(pad[:, :], table[:, 0, :], 0.0, 8192.0, ALU.is_equal, ALU.mult))
            link(nc.vector.tensor_tensor(sidxf[:, :], table[:, 0, :], pad[:, :], ALU.add))
            nc.vector.tensor_scalar(sidx[:, :], sidxf[:, :], 1.0, None, ALU.subtract).then_inc(table_ready, 1)

            def copy_rows(par):
                nc.vector.tensor_copy(xs0[par][:, :], bank[6][:, 0:P])
                nc.vector.tensor_copy(xs1[par][0:C1, :], bank[6][0:C1, P:2 * P]).then_inc(xt_copied, 1)

            for b in range(BATCH):
                dve.wait_ge(init_psum, b + 1)
                nc.vector.tensor_tensor(out_init[:, 2 * b:2 * b + 2, :],
                                        bank[2 + b][:, 0:2 * MODEL].rearrange("p (t c) -> p t c", t=2),
                                        h2[:, 2 * b:2 * b + 2, :], ALU.add).then_inc(init_sb, 1)
            for j in range(2):
                dve.wait_ge(xt_psum, j + 1)
                copy_rows(j)
            dve.sem_inc(y_free, 1)
            dve.wait_ge(table_ready, 1)
            used = dve.value_load(tiles_used[0:1, 0:1], min_val=1, max_val=SLOT_TILES)
            with dve.Fori(0, (SLOT_TILES + 1) // 2) as i:
                for par in range(2):
                    with dve.If(2 * i + par < used):
                        j = 2 * i + par
                        dve.wait_ge(ht_psum, j + 1)
                        nc.vector.tensor_copy(hid_t[:, FK // 2:FK, :], bank[5][:, 0:NH]).then_inc(ht_dve, 1)
                        dve.wait_ge(xt_psum, j + 3)
                        copy_rows(par)
                        dve.wait_ge(ys_free, j + 1)
                        dve.wait_ge(y_psum, j + 1)
                        nc.vector.tensor_scalar(ys[par][:, :], bank[7][:, 0:MODEL], slot_w[:, bass.ds(j, 1)], None,
                                                ALU.mult).then_inc(y_ready, 1)
                        dve.wait_ge(y_ready, j + 1)
                        dve.sem_inc(y_free, 1)

        @block.tensor
        def _(pe):
            pe.wait_ge(attn_in, 16 * 6)
            for bank_n, cols in ((6, slice(0, C0)), (7, slice(C0, MODEL + 1))):
                m = cols.stop - cols.start
                for (lhs, rhs), first in (((wq0, wk0), True), ((wq1, wk1), False)):
                    last = nc.tensor.matmul(bank[bank_n][0:m, 256:257 + MODEL], lhs[:, cols], rhs[:, :],
                                            start=first, stop=not first)
            last.then_inc(qk_psum, 1)
            pe.wait_ge(xtab_ready, 1)

            def pick(n):
                level, col, width, piece = pieces[n]
                if n >= 2:
                    pe.wait_ge(picked_sb, n - 1)
                for k in range(2):
                    pe.wait_ge(onehot_ready, 2 * n + k + 1)
                    for part, tab in enumerate((xtab_hi, xtab_lo)):
                        last = nc.tensor.matmul(bank[n % 2][0:ROWS, 0:width], tab[:, 2 * level + k, :],
                                                onehot[:, n % 2, k, 0:width],
                                                start=(k == 0 and part == 0), stop=(k == 1 and part == 1))
                last.then_inc(picked_psum, 1)

            def small_level(level, col):
                nt = LEVEL_TOKENS[level]
                for g in range(GROUP):
                    for b in range(BATCH):
                        r = slice(B1 * b, B1 * b + GATHER_ROWS)
                        c = START[level] + g * nt
                        last = nc.tensor.matmul(bank[2 + b][0:nt, col:col + EMBED], gathered[r, c:c + nt],
                                                we_sb[r, level, g, :], start=(g == 0), stop=(g == GROUP - 1))
                last.then_inc(tok_psum, 1)

            def fine_level(groups):
                for g in groups:
                    for b in range(BATCH):
                        r = slice(B1 * b, B1 * b + GATHER_ROWS)
                        c = START[0] + g * SEQ
                        last = nc.tensor.matmul(bank[4 + b][B1 * b:B1 * b + EMBED, 0:SEQ], we_sb[r, 0, g, :],
                                                gathered[r, c:c + SEQ], start=(g == 0), stop=(g == GROUP - 1))
                return last

            pick(0)
            pick(1)
            pe.wait_ge(we_in, 16 * 2 * (1 + 4 + 16))
            pe.wait_ge(picked_sb, 1)
            small_level(2, EMBED)
            pick(2)
            pick(3)
            pe.wait_ge(picked_sb, 3)
            pe.wait_ge(tok_sb, 2)
            small_level(1, 0)
            pe.wait_ge(qk_sb, 2)
            pe.wait_ge(tok_sb, 2)
            nc.tensor.matmul(bank[7][:, 0:SEQ], t12[0:LEVEL_TOKENS[2], 1, :],
                             K[0:LEVEL_TOKENS[2], K_UP2:K_UP2 + SEQ], start=True, stop=True).then_inc(cat_psum, 1)
            pe.wait_ge(tok_sb, 4)
            nc.tensor.matmul(bank[6][:, 0:SEQ], t12[0:LEVEL_TOKENS[1], 0, :],
                             K[0:LEVEL_TOKENS[1], K_UP1:K_UP1 + SEQ], start=True, stop=True).then_inc(cat_psum, 1)
            for n in range(4, len(pieces)):
                pick(n)
                pe.wait_ge(picked_sb, n)
                last = fine_level(range(2 * (n - 4), 2 * (n - 3)))
            pe.wait_ge(picked_sb, len(pieces))
            fine_level(range(2 * (len(pieces) - 4), GROUP)).then_inc(cat_psum, 1)
            pe.wait_ge(wf_in, 16 * 5)
            pe.wait_ge(cat_sb, 4)
            for b in range(BATCH):
                r = slice(B1 * b, B1 * b + EMBED)
                for half in range(2):
                    for level in range(LEVELS):
                        last = nc.tensor.matmul(bank[b][:, MODEL * half:MODEL * (half + 1)],
                                                cat[r, level, P * half:P * (half + 1)], wf_sb[r, level, :],
                                                start=(level == 0), stop=(level == LEVELS - 1))
                last.then_inc(h_psum, 1)

            def transposes(src, done, bank0, signal):
                for b in range(BATCH):
                    for half in range(2):
                        t = 2 * b + half
                        pe.wait_ge(done, t + 1)
                        c = P * half
                        nc.tensor.transpose(bank[bank0 + b][:, c:c + P], src[:, t, 0:C0], ident)
                        last = nc.tensor.transpose(bank[bank0 + b][0:C1, SEQ + c:SEQ + c + P], src[:, t, C0:MODEL],
                                                   ident)
                    last.then_inc(signal, 1)

            transposes(z, z_ready, 2, zt_psum)
            pe.wait_ge(zt_sb, 2)
            for n, (bank_n, cols) in enumerate(((6, slice(0, C0)), (7, slice(C0, MODEL + 1)))):
                m = cols.stop - cols.start
                nc.tensor.matmul(bank[bank_n][0:m, :], qk0[:, cols], zt0[:, :], start=True, stop=False)
                nc.tensor.matmul(bank[bank_n][0:m, :], qk1[:, cols], zt1[:, :], start=False,
                                 stop=True).then_inc(q_psum, 1)
            for t in range(TOKEN_TILES):
                o = bank[4 + t // 2][:, MODEL * (t % 2):MODEL * (t % 2 + 1)]
                nc.tensor.matmul(o, zt0[:, P * t:P * (t + 1)], wv0[:, :], start=True, stop=False)
                last = nc.tensor.matmul(o, zt1[:, P * t:P * (t + 1)], wv1[:, :], start=False, stop=True)
                if t % 2:
                    last.then_inc(v_psum, 1)
            pe.wait_ge(q_sb, 2)
            for t in range(TOKEN_TILES):
                b = t // 2
                o = bank[b][:, SEQ * (t % 2):SEQ * (t % 2 + 1)]
                nc.tensor.matmul(o, qt0[:, P * t:P * (t + 1)], zt0[:, SEQ * b:SEQ * (b + 1)], start=True, stop=False)
                last = nc.tensor.matmul(o, qt1[:, P * t:P * (t + 1)], zt1[:, SEQ * b:SEQ * (b + 1)],
                                        start=False, stop=True)
                if t % 2:
                    last.then_inc(score_psum, 1)
            for t in range(TOKEN_TILES):
                pe.wait_ge(probs_ready, t + 1)
                for k in range(2):
                    c = P * (2 * (t % 2) + k)
                    last = nc.tensor.transpose(bank[2 + t // 2][:, c:c + P], probs[:, t, P * k:P * (k + 1)], ident)
                if t % 2:
                    last.then_inc(pt_psum, 1)
            pe.wait_ge(v_ready, 2)
            pe.wait_ge(pt_sb, 2)
            for t in range(TOKEN_TILES):
                o = bank[4 + t // 2][:, MODEL * (t % 2):MODEL * (t % 2 + 1)]
                for k in range(2):
                    last = nc.tensor.matmul(o, probs_t[:, t, k, :], v_sb[:, 2 * (t // 2) + k, :],
                                            start=(k == 0), stop=(k == 1))
                if t % 2:
                    last.then_inc(pv_psum, 1)
            transposes(z2, z2_ready, 6, z2t_psum)
            pe.wait_ge(z2t_sb, 2)
            pe.wait_ge(misc_in, 48)
            for t in range(TOKEN_TILES):
                o = bank[0][:, EXPERTS * t:EXPERTS * (t + 1)]
                nc.tensor.matmul(o, z2t0[:, P * t:P * (t + 1)], rw0[:, :], start=True, stop=False)
                last = nc.tensor.matmul(o, z2t1[:, P * t:P * (t + 1)], rw1[:, :], start=False, stop=True)
            last.then_inc(logit_psum, 1)
            pe.wait_ge(gp_set, 6)
            pe.wait_ge(member_ready, 1)
            memb = member[:, :, :].rearrange("p t e -> p (t e)")
            nc.tensor.matmul(bank[4][:, 0:32], tri_b[:, :], memb, start=True, stop=False, skip_group_check=True)
            for t in range(1, TOKEN_TILES):
                nc.tensor.matmul(bank[4][:, EXPERTS * t:32], ones_b[:, :], memb[:, 0:32 - EXPERTS * t],
                                 start=False, stop=False, skip_group_check=True)
            for t in range(TOKEN_TILES):
                last = nc.tensor.matmul(bank[4][:, 32:32 + EXPERTS], ones_b[:, :],
                                        memb[:, EXPERTS * t:EXPERTS * (t + 1)],
                                        start=False, stop=(t == TOKEN_TILES - 1), skip_group_check=True)
            last.then_inc(rank_psum, 1)
            pe.wait_ge(comb_ready, 1)
            for t in range(TOKEN_TILES):
                last = nc.tensor.transpose(bank[1][0:EXPERTS, P * t:P * (t + 1)], comb[:, t, :], ident)
            last.then_inc(comb_psum, 1)
            pe.wait_ge(payload_ready, 1)
            for c in range(2 * TOKEN_TILES):
                last = nc.tensor.matmul(bank[5][:, 0:3 * TABLE], in_row[:, c, :],
                                        payload[:, c, :, :].rearrange("p v t -> p (v t)"),
                                        start=(c == 0), stop=(c == 2 * TOKEN_TILES - 1))
            last.then_inc(table_psum, 1)
            pe.wait_ge(comb_sb, 1)
            for t in range(TOKEN_TILES):
                last = nc.tensor.matmul(bank[2 + t // 2][:, MODEL * (t % 2):MODEL * (t % 2 + 1)],
                                        comb_t[:, P * t:P * (t + 1)], b2_sb[:, :], start=True, stop=True)
                if t % 2:
                    last.then_inc(init_psum, 1)

            def transpose_rows(par):
                nc.tensor.transpose(bank[6][:, 0:P], xg[par][:, 0:C0], ident)
                nc.tensor.transpose(bank[6][0:C1, P:2 * P], xg[par][:, C0:MODEL], ident).then_inc(xt_psum, 1)

            def up(e, par):
                for n in range(2):
                    at = e * HIDDEN + n * NH
                    nc.tensor.matmul(bank[2 * par + n][:, 0:NH], xs0[par][:, :], w1_0[:, bass.ds(at, NH)],
                                     start=True, stop=False)
                    last = nc.tensor.matmul(bank[2 * par + n][:, 0:NH], xs1[par][:, :], w1_1[:, bass.ds(at, NH)],
                                            start=False, stop=True)
                last.then_inc(up_psum, 1)

            for j in range(2):
                pe.wait_ge(gather_done, 16 * (j + 1))
                if j:
                    pe.wait_ge(xt_copied, j)
                transpose_rows(j)
            pe.wait_ge(init_sb, 2)
            pe.wait_ge(table_ready, 1)
            pe.wait_ge(moe_in, 16 * (3 * EXPERTS + 1))
            used = pe.value_load(tiles_used[0:1, 0:1], min_val=1, max_val=SLOT_TILES)
            first = pe.value_load(expert[0:1, 0:1], min_val=0, max_val=EXPERTS - 1)
            pe.wait_ge(xt_copied, 1)
            up(first, 0)
            with pe.Fori(0, (SLOT_TILES + 1) // 2) as i:
                for par in range(2):
                    with pe.If(2 * i + par < used):
                        j = 2 * i + par
                        nxt = pe.value_load(expert[0:1, bass.ds(j + 1, 1)], min_val=0, max_val=EXPERTS - 1)
                        own = pe.value_load(expert[0:1, bass.ds(j, 1)], min_val=0, max_val=EXPERTS - 1)
                        pe.wait_ge(xt_copied, j + 2)
                        up(nxt, (par + 1) % 2)
                        pe.wait_ge(gelu_done, j + 1)
                        for k in range(FK):
                            c = P * (k % 3)
                            last = nc.tensor.transpose(bank[4 + k // 3][:, c:c + P], hid[:, k * P:(k + 1) * P], ident)
                        last.then_inc(ht_psum, 1)
                        pe.wait_ge(gather_done, 16 * j + 48)
                        transpose_rows(par)
                        pe.wait_ge(ht_act, j + 1)
                        pe.wait_ge(ht_dve, j + 1)
                        pe.wait_ge(y_free, j + 1)
                        for k in range(FK):
                            last = nc.tensor.matmul(bank[7][:, 0:MODEL], hid_t[:, k, :],
                                                    w2_sb[:, bass.ds(own * (FK * MODEL) + k * MODEL, MODEL)],
                                                    start=(k == 0), stop=(k == FK - 1))
                        last.then_inc(y_psum, 1)


def kernel(**inputs):
    import concourse.bacc as bacc
    from concourse.bass_utils import run_bass_kernel_spmd

    a = {k: np.asarray(v) for k, v in inputs.items()}
    x = a["x"]

    tables = []
    for level, p in enumerate((1, 2, 4)):
        side = IMAGE // p
        t = x.reshape(BATCH, CHANNELS, side, p, side, p).transpose(2, 4, 0, 3, 5, 1)
        t = t.reshape(PATCHES[level] // LOW, 2, P, BATCH, FEATURES[level])
        tables.append(t.transpose(2, 1, 3, 0, 4).reshape(P, 2, 1, BATCH * GATHER_ROWS))
    xt = np.concatenate(tables, axis=2).transpose(0, 2, 1, 3).reshape(P, 2 * LEVELS, BATCH * GATHER_ROWS)
    idx = np.concatenate([a[f"L0_tok_idx{level}"].reshape(-1, GROUP).T.reshape(-1) for level in (2, 1, 0)])
    arrays = {"xt": xt, "idx": idx}
    for level in range(LEVELS):
        w = a[f"L0_tok_W{level}"].reshape(EMBED, GROUP, FEATURES[level])
        arrays[f"we{level}"] = w.transpose(2, 1, 0)
    arrays["embed_bias"] = np.stack([a[f"L0_tok_b{level}"] for level in range(LEVELS)], axis=1)
    arrays["wf"] = a["L0_tok_Wf"].T.reshape(LEVELS, EMBED, MODEL).transpose(1, 0, 2)
    arrays["bf"] = a["L0_tok_bf"]
    arrays["wq"] = np.concatenate([a["L0_attn_Wq"], a["L0_attn_bq"][:, None]], axis=1)
    arrays["wk"] = np.concatenate([a["L0_attn_Wk"], a["L0_attn_bk"][:, None]], axis=1)
    arrays["wv"] = np.concatenate([a["L0_attn_Wv"].T, a["L0_attn_bv"][None, :]], axis=0)
    arrays["router"] = a["L0_ffn_router_w"].T
    arrays["w1"], arrays["b1"] = a["L0_ffn_w1"], a["L0_ffn_b1"].reshape(1, EXPERTS * HIDDEN)
    arrays["w2"], arrays["b2"] = a["L0_ffn_w2"], a["L0_ffn_b2"]

    k = np.zeros((P, K_END), np.float32)
    p = np.arange(P)
    k[:, K_IDENT:K_TRI] = np.eye(P)
    k[:, K_TRI:K_IOTA] = p[:, None] < p[None, :]
    k[:, K_IOTA:K_UP1] = p[None, :]
    for level, col in ((1, K_UP1), (2, K_UP2)):
        n = LEVEL_TOKENS[level]
        pos = np.clip((np.arange(SEQ, dtype=np.float32) + 0.5) * (n / SEQ) - 0.5, 0.0, n - 1)
        lo = np.floor(pos).astype(int)
        hi = np.minimum(lo + 1, n - 1)
        up = np.zeros((n, SEQ), np.float32)
        np.add.at(up, (lo, np.arange(SEQ)), 1.0 - (pos - lo))
        np.add.at(up, (hi, np.arange(SEQ)), pos - lo)
        k[:n, col:col + SEQ] = up
    k[:, K_LOW], k[:, K_LOW + 1] = p, p + P
    for level in range(LEVELS):
        k[:, K_HIGH + level] = (p % B1) // FEATURES[level]
    for t in range(TOKEN_TILES):
        k[:, K_TOKEN + t] = t * P + p + 1
    k[:, K_HALF:K_END] = -0.5
    arrays["consts"] = k

    nc = bacc.Bacc("TRN2", target_bir_lowering=False, num_devices=1)
    aps, feeds = {}, {}
    for name, array in arrays.items():
        array = np.ascontiguousarray(array)
        feeds[f"in_{name}"] = array
        aps[name] = nc.dram_tensor(f"in_{name}", array.shape, mybir.dt.from_np(array.dtype), kind="ExternalInput").ap()
    out = nc.dram_tensor("out", (TOKENS, MODEL), mybir.dt.float32, kind="ExternalOutput").ap()
    build(nc, aps["xt"], aps["idx"], [aps[f"we{level}"] for level in range(LEVELS)], aps["embed_bias"], aps["wf"],
          aps["bf"], aps["wq"], aps["wk"], aps["wv"], aps["router"], aps["w1"], aps["b1"], aps["w2"], aps["b2"],
          aps["consts"], out)
    result = run_bass_kernel_spmd(nc, [feeds], core_ids=[0])
    return result.results[0]["out"].reshape(BATCH, SEQ, MODEL)
```

```python
import numpy as np
import concourse.bass as bass
from concourse import mybir
from contextlib import ExitStack

BATCH, CHANNELS, IMAGE = 2, 3, 64
GROUP = 16
EMBED, LEVELS = 64, 3
MODEL = EMBED * LEVELS
EXPERTS, HIDDEN = 8, 768
SEQ = IMAGE * IMAGE // GROUP
TOKENS = BATCH * SEQ
PATCHES = [4096, 1024, 256]
LEVEL_TOKENS = [n // GROUP for n in PATCHES]
FEATURES = [3, 12, 48]
P = 128
LOW = 256
GATHER_ROWS = 48
B1 = 64
ROWS = B1 + GATHER_ROWS
PICKS = sum(PATCHES)
START = [PATCHES[1] + PATCHES[2], PATCHES[2], 0]
TOKEN_TILES = TOKENS // P
C0, C1 = P, MODEL - P
SLOT_TILES = 2 * TOKENS // P + EXPERTS - 1
AHEAD = 3
TABLE = 2 * ((SLOT_TILES + AHEAD) // 2 + 1)
FK = HIDDEN // P
NH = HIDDEN // 2
EPS = 1e-5

K_LOW = 0
K_HIGH = K_LOW + 2
K_TOKEN = K_HIGH + LEVELS
K_HALF = K_TOKEN + TOKEN_TILES
K_IDENT = K_HALF + TOKEN_TILES + 3
K_TRI = K_IDENT + P
K_IOTA = K_TRI + P
K_UP1 = K_IOTA + P
K_UP2 = K_UP1 + SEQ
K_END = K_UP2 + SEQ
A_Q, A_K, A_V, A_R = 0, MODEL + 1, 2 * (MODEL + 1), 3 * MODEL + 2
A_END = A_R + EXPERTS


def build(nc, xt, idx, we, fuse, bf, attn, w1, b1, w2, b2, consts, out):
    F, R, I32, U32, U8, BF = (mybir.dt.float32, mybir.dt.float32r, mybir.dt.int32, mybir.dt.uint32,
                              mybir.dt.uint8, mybir.dt.bfloat16)
    ALU, ACT, AX = mybir.AluOpType, mybir.ActivationFunctionType, mybir.AxisListType
    ctx = ExitStack()
    with ctx:
        def sb(name, shape, dt=F):
            return ctx.enter_context(nc.sbuf_tensor(name, shape, dt))

        def sem(name):
            return ctx.enter_context(nc.semaphore(name))

        z2_dram = nc.dram_tensor("z2_dram", (TOKENS, MODEL), F).ap()

        K = sb("K", [P, K_END])
        ident, tri, iota = K[:, K_IDENT:K_TRI], K[:, K_TRI:K_IOTA], K[:, K_IOTA:K_UP1]
        xtab = sb("xtab", [P, 2 * LEVELS, ROWS])
        xtab_hi = sb("xtab_hi", [P, 2 * LEVELS, ROWS], R)
        xtab_lo = sb("xtab_lo", [P, 2 * LEVELS, ROWS], R)
        picks = sb("picks", [P, PICKS], I32)
        pick_bytes = picks[:, :].bitcast(U8).rearrange("p (j f) -> p j f", f=4)
        onehot = sb("onehot", [P, 2, 2, 512], R)
        gathered = sb("gathered", [P, PICKS])
        old_picks, old_gathered = picks[:, :].bitcast(F), gathered[:, :]

        def cut(space, start, *dims):
            view = space[:, start:start + int(np.prod(dims))]
            names = " ".join("abc"[:len(dims)])
            return view.rearrange(f"p ({names}) -> p {names}", **dict(zip("abc", dims))) if len(dims) > 1 else view

        probs = cut(old_picks, 0, TOKEN_TILES, SEQ)
        probs_t = cut(old_picks, 1024, TOKEN_TILES, 2, P)
        qt0 = cut(old_picks, 2048, TOKENS)
        qt1 = cut(old_picks, 2560, TOKENS)[0:C1 + 1]
        v_sb = cut(old_picks, 3072, TOKEN_TILES, MODEL)
        out_init = cut(old_picks, 3840, TOKEN_TILES, MODEL)
        z2t0 = cut(old_gathered, 0, TOKENS)
        z2t1 = cut(old_gathered, 512, TOKENS)[0:C1]
        z2 = cut(old_gathered, 1024, TOKEN_TILES, MODEL)
        in_row = onehot[:, :, :, :].rearrange("p a b (c r) -> p (a b c) r", r=P)[:, 0:2 * TOKEN_TILES, :]
        we_sb = sb("we_sb", [P, LEVELS, GROUP, EMBED])
        fuse_sb = sb("fuse_sb", [P, LEVELS * (MODEL + 1)])
        wf_sb = fuse_sb[:, 0:LEVELS * MODEL].rearrange("p (l c) -> p l c", l=LEVELS)
        ebias = fuse_sb[:, LEVELS * MODEL:LEVELS * (MODEL + 1)]
        t12 = sb("t12", [B1, 2, P])
        cat = sb("cat", [P, LEVELS, SEQ])
        bf_sb = sb("bf_sb", [P, MODEL])
        attn0, attn1 = sb("attn0", [C0, A_END]), sb("attn1", [C1 + 1, A_END])
        wq0, wq1 = attn0[:, A_Q:A_K], attn1[0:C1, A_Q:A_K]
        wk0, wk1 = attn0[:, A_K:A_V], attn1[0:C1, A_K:A_V]
        wv0, wv1 = attn0[:, A_V:A_R], attn1[:, A_V:A_R]
        rw0, rw1 = attn0[:, A_R:A_END], attn1[0:C1, A_R:A_END]
        qk0, qk1 = sb("qk0", [C0, MODEL + 1]), sb("qk1", [C1 + 1, MODEL + 1])
        h = sb("h", [P, TOKEN_TILES, MODEL])
        stats = sb("stats", [P, TOKEN_TILES, 6])
        mv = sb("mv", [P, TOKEN_TILES, 2])
        vareps = sb("vareps", [P, TOKEN_TILES])
        rstd = sb("rstd", [P, TOKEN_TILES])
        z = sb("z", [P, TOKEN_TILES, MODEL])
        zt0, zt1 = sb("zt0", [C0, TOKENS]), sb("zt1", [C1 + 1, TOKENS])
        nmax = sb("nmax", [P, TOKEN_TILES])
        esum = sb("esum", [P, TOKEN_TILES])
        rsum = sb("rsum", [P, TOKEN_TILES])
        h2 = sb("h2", [P, TOKEN_TILES, MODEL])
        b2_sb = sb("b2_sb", [EXPERTS, MODEL])
        ones_b = sb("ones_b", [P, 512], BF)
        tri_b = sb("tri_b", [P, P], BF)
        ones8 = sb("ones8", [P, EXPERTS])
        logits = sb("logits", [P, TOKEN_TILES, EXPERTS])
        top = sb("top", [P, TOKEN_TILES, EXPERTS])
        topi = sb("topi", [P, TOKEN_TILES, EXPERTS], U32)
        topf = sb("topf", [P, 2, TOKEN_TILES])
        gap = sb("gap", [P, TOKEN_TILES])
        egap = sb("egap", [P, TOKEN_TILES])
        eden = sb("eden", [P, TOKEN_TILES])
        wgt = sb("wgt", [P, 2, TOKEN_TILES])
        chosen = sb("chosen", [P, 2, TOKEN_TILES, EXPERTS])
        member = sb("member", [P, TOKEN_TILES, EXPERTS], BF)
        cnti = sb("cnti", [P, EXPERTS], I32)
        ntile = sb("ntile", [P, EXPERTS], I32)
        tile_end = sb("tile_end", [P, EXPERTS])
        base = sb("base", [P, EXPERTS])
        slot = sb("slot", [P, TOKEN_TILES, EXPERTS])
        picked = sb("picked", [P, 2, TOKEN_TILES, EXPERTS])
        slotf = sb("slotf", [P, 2 * TOKEN_TILES])
        sloti = sb("sloti", [P, 2 * TOKEN_TILES], I32)
        slot_tile = sb("slot_tile", [P, 2 * TOKEN_TILES], I32)
        slot_row = sb("slot_row", [P, 2 * TOKEN_TILES], I32)
        in_tile = sb("in_tile", [P, 2 * TOKEN_TILES, TABLE])
        payload = sb("payload", [P, 2 * TOKEN_TILES, 3, TABLE], R)
        values = sb("values", [P, 2 * TOKEN_TILES, 3])
        wgt_hi = sb("wgt_hi", [P, 2 * TOKEN_TILES], R)
        table = sb("table", [P, 3, TABLE])
        slot_w = sb("slot_w", [P, TABLE])
        gidx = sb("gidx", [P, TABLE], I32)
        pad = sb("pad", [P, TABLE])
        sidxf = sb("sidxf", [P, TABLE])
        sidx = sb("sidx", [P, TABLE], I32)
        before = sb("before", [P, TABLE, EXPERTS])
        expertf = sb("expertf", [P, TABLE])
        expert = sb("expert", [P, TABLE], I32)
        tiles_used = sb("tiles_used", [P, 1], I32)
        comb = sb("comb", [P, TOKEN_TILES, EXPERTS])
        comb2 = sb("comb2", [P, TOKEN_TILES, EXPERTS])
        comb_t = sb("comb_t", [EXPERTS, TOKENS])
        w1_0 = sb("w1_0", [C0, EXPERTS * HIDDEN])
        w1_1 = sb("w1_1", [C1 + 1, EXPERTS * HIDDEN])
        w2_sb = sb("w2_sb", [P, EXPERTS * FK * MODEL])
        gi_col = [sb(f"gi_col{i}", [P, 1], I32) for i in range(2)]
        si_col = [sb(f"si_col{i}", [P, 1], I32) for i in range(2)]
        xg = [sb(f"xg{i}", [P, MODEL]) for i in range(2)]
        xs0 = [sb(f"xs0_{i}", [C0, P]) for i in range(2)]
        xs1 = [sb(f"xs1_{i}", [C1 + 1, P]) for i in range(2)]
        hid = sb("hid", [P, HIDDEN])
        hid_t = sb("hid_t", [P, FK, P])
        ys = [sb(f"ys{i}", [P, MODEL]) for i in range(2)]

        bank = [ctx.enter_context(nc.psum_tensor(f"bank{i}", [P, 512], F)) for i in range(8)]

        k_in, kmat_in, x_in, wf_in = sem("k_in"), sem("kmat_in"), sem("x_in"), sem("wf_in")
        we_in = [sem(f"we_in{level}") for level in range(LEVELS)]
        attn_in, misc_in, moe_in = sem("attn_in"), sem("misc_in"), sem("moe_in")
        pick_in = [sem(f"pick_in{i}") for i in range(4)]
        ones_ready, dv, gp_set = sem("ones_ready"), sem("dv"), sem("gp_set")
        xtab_ready, onehot_ready, picked_psum, picked_sb = (sem("xtab_ready"), sem("onehot_ready"),
                                                            sem("picked_psum"), sem("picked_sb"))
        tok_psum, tok_sb, cat_psum, cat_sb = sem("tok_psum"), sem("tok_sb"), sem("cat_psum"), sem("cat_sb")
        qk_psum, qk_sb = sem("qk_psum"), sem("qk_sb")
        h_psum, h_ready, var_ready, rstd_ready = sem("h_psum"), sem("h_ready"), sem("var_ready"), sem("rstd_ready")
        z_ready, zt_psum, zt_sb = sem("z_ready"), sem("zt_psum"), sem("zt_sb")
        v_psum, v_ready, q_psum, q_sb = sem("v_psum"), sem("v_ready"), sem("q_psum"), sem("q_sb")
        score_psum, nmax_ready, probs_ready = sem("score_psum"), sem("nmax_ready"), sem("probs_ready")
        pt_psum, pt_sb, pv_psum = sem("pt_psum"), sem("pt_sb"), sem("pv_psum")
        var2_ready, rstd2_ready, z2_ready = sem("var2_ready"), sem("rstd2_ready"), sem("z2_ready")
        z2_stored, z2t_psum, z2t_sb, logit_psum = sem("z2_stored"), sem("z2t_psum"), sem("z2t_sb"), sem("logit_psum")
        gap_ready, egap_ready, member_ready, rank_psum = (sem("gap_ready"), sem("egap_ready"),
                                                          sem("member_ready"), sem("rank_psum"))
        gidx_ready, expert_ready = sem("gidx_ready"), sem("expert_ready")
        payload_ready, table_psum, table_ready = sem("payload_ready"), sem("table_psum"), sem("table_ready")
        comb_ready, comb_psum, comb_sb, init_psum, init_sb = (sem("comb_ready"), sem("comb_psum"), sem("comb_sb"),
                                                              sem("init_psum"), sem("init_sb"))
        out_stored = sem("out_stored")
        column_ready, scatter_column_ready = sem("column_ready"), sem("scatter_column_ready")
        xt_psum, xt_copied = sem("xt_psum"), sem("xt_copied")
        gather_done = [sem(f"gather_done{i}") for i in range(2)]
        up_psum, gelu_done, ht_psum, ht_act, ht_dve = (sem("up_psum"), sem("gelu_done"), sem("ht_psum"),
                                                       sem("ht_act"), sem("ht_dve"))
        y_psum, y_free, ys_free, y_ready, scatter_done, pool_mark = (sem("y_psum"), sem("y_free"), sem("ys_free"), sem("y_ready"),
                                                            sem("scatter_done"), sem("pool_mark"))

        pieces = [(2, START[2], PATCHES[2], 0)]
        pieces += [(1, START[1] + 512 * i, 512, 1) for i in range(PATCHES[1] // 512)]
        pieces += [(0, START[0] + 512 * i, 512, 2 + i // 4) for i in range(PATCHES[0] // 512)]
        piece_span = [(0, START[1]), (START[1], START[0]), (START[0], START[0] + 2048), (START[0] + 2048, PICKS)]

        def tokens(b, half):
            return (2 * b + half) * P

        block = ctx.enter_context(nc.Block())

        @block.sync
        def _(sp):
            xin = xt.rearrange("p t (b r) -> p t b r", b=2)
            for b in range(BATCH):
                sp.dma_start(xtab[:, :, B1 * b:B1 * b + GATHER_ROWS], xin[:, :, b, :]).then_inc(x_in, 16)
            for n, (lo, hi) in enumerate(piece_span):
                sp.dma_start(picks[:, lo:hi], idx[lo:hi].partition_broadcast(P)).then_inc(pick_in[n], 16)
            for e in range(0, EXPERTS, 2):
                w1e = w1[e:e + 2, :, :].rearrange("e c f -> c e f")
                at = slice(e * HIDDEN, (e + 2) * HIDDEN)
                sp.dma_start(w1_0[:, at].rearrange("p (e f) -> p e f", e=2), w1e[0:C0, :, :]).then_inc(moe_in, 16)
                sp.dma_start(w1_1[0:C1, at].rearrange("p (e f) -> p e f", e=2),
                             w1e[C0:MODEL, :, :]).then_inc(moe_in, 16)
                sp.dma_start(w2_sb[:, e * FK * MODEL:(e + 2) * FK * MODEL].rearrange("p (k c) -> p k c", c=MODEL),
                             w2[e:e + 2, :, :].rearrange("e (k p) c -> p (e k) c", p=P)).then_inc(moe_in, 16)
            sp.dma_start(w1_1[C1:C1 + 1, :], b1).then_inc(moe_in, 16)
            for t in range(TOKEN_TILES):
                sp.wait_ge(z2_ready, t + 1)
                sp.dma_start(z2_dram[t * P:(t + 1) * P, :], z2[:, t, :]).then_inc(z2_stored, 16)
            for b in range(BATCH):
                sp.wait_ge(init_sb, b + 1)
                sp.dma_start(out.rearrange("(t p) c -> p t c", p=P)[:, 2 * b:2 * b + 2, :],
                             out_init[:, 2 * b:2 * b + 2, :]).then_inc(out_stored, 16)
            sp.wait_ge(out_stored, 16 * BATCH)

        @block.gpsimd
        def _(pool):
            for level in (2, 1, 0):
                highs, f = GATHER_ROWS // FEATURES[level], FEATURES[level]
                src = we[level].rearrange("f g e -> f (g e)")
                for b in range(BATCH):
                    dst = we_sb[B1 * b:B1 * b + GATHER_ROWS, level, :, :].rearrange("r g e -> r (g e)")
                    pool.dma_start(dst, src if highs == 1 else src[None, :, :].to_broadcast(
                        [highs, f, GROUP * EMBED])).then_inc(we_in[level], 16)
            pool.wait_ge(kmat_in, 16)
            nc.gpsimd.tensor_copy(tri_b[:, :], tri).then_inc(gp_set, 1)
            half = K[:, K_HALF:K_HALF + TOKEN_TILES]
            pool.wait_ge(var_ready, 1)
            nc.gpsimd.tensor_tensor(rstd[:, :], vareps[:, :], half, ALU.pow).then_inc(rstd_ready, 1)
            pool.wait_ge(var2_ready, 1)
            nc.gpsimd.tensor_tensor(rstd[:, :], vareps[:, :], half, ALU.pow).then_inc(rstd2_ready, 1)

            def gather_column(j, par):
                nc.gpsimd.tensor_copy(gi_col[par][:, :], gidx[:, bass.ds(j, 1)]).then_inc(column_ready, 1)

            def gather(par):
                nc.gpsimd.indirect_dma_start(
                    out=xg[par][:, :], out_offset=None, in_=z2_dram,
                    in_offset=bass.IndirectOffsetOnAxis(gi_col[par][:, 0:1].bitcast(U32), 0)
                ).then_inc(gather_done[par], 16)

            def scatter_column(j, par):
                nc.gpsimd.tensor_copy(si_col[par][:, :], sidx[:, bass.ds(j, 1)]).then_inc(scatter_column_ready, 1)

            def scatter(par):
                nc.gpsimd.indirect_dma_start(
                    out=out, out_offset=bass.IndirectOffsetOnAxis(si_col[par][:, 0:1].bitcast(U32), 0),
                    in_=ys[par][:, :], in_offset=None, bounds_check=TOKENS - 1, oob_is_err=False,
                    compute_op=ALU.add).then_inc(scatter_done, 16)

            def waited():
                pool.sem_inc(pool_mark, 1)

            pool.wait_ge(gidx_ready, 1)
            pool.wait_ge(z2_stored, 16 * TOKEN_TILES)
            for j in range(AHEAD):
                if j >= 2:
                    pool.wait_ge(xt_psum, j - 1)
                gather_column(j, j % 2)
                pool.wait_ge(column_ready, j + 1)
                gather(j % 2)
            pool.sem_inc(ys_free, 2)
            pool.wait_ge(expert_ready, 1)
            used = pool.value_load(tiles_used[0:1, 0:1], min_val=2, max_val=SLOT_TILES)
            pool.wait_ge(table_ready, 1)
            pool.wait_ge(out_stored, 16 * BATCH)
            with pool.Fori(0, (SLOT_TILES + 1) // 2) as i:
                for par in range(2):
                    j = 2 * i + par
                    with pool.If(j < used):
                        with pool.If(j + 1 < used):
                            pool.wait_ge(xt_psum, j + 2)
                            waited()
                            gather_column(j + AHEAD, 1 - par)
                            pool.wait_ge(column_ready, j + AHEAD + 1)
                            waited()
                            gather(1 - par)
                            waited()
                        scatter_column(j, par)
                        pool.wait_ge(scatter_column_ready, j + 1)
                        waited()
                        pool.wait_ge(y_ready, j + 1)
                        waited()
                        scatter(par)
                        pool.wait_ge(scatter_done, 16 * j + 16)
                        pool.sem_inc(ys_free, 1)
            pool.wait_ge(gather_done[0], 16 * ((used + 3) // 2))
            waited()
            pool.wait_ge(gather_done[1], 16 * ((used + 2) // 2))
            waited()

        @block.scalar
        def _(act):
            act.dma_start(K[:, 0:K_IDENT], consts[:, 0:K_IDENT]).then_inc(k_in, 16)
            act.dma_start(attn0[:, :], attn[0:C0, :]).then_inc(attn_in, 16)
            act.dma_start(attn1[:, :], attn[C0:MODEL + 1, :]).then_inc(attn_in, 16)
            act.dma_start(K[:, K_IDENT:K_END], consts[:, K_IDENT:K_END]).then_inc(kmat_in, 16)
            for b in range(BATCH):
                act.dma_start(fuse_sb[B1 * b:B1 * b + EMBED, :], fuse).then_inc(wf_in, 16)
            act.dma_start(bf_sb[:, :], bf.partition_broadcast(P)).then_inc(wf_in, 16)
            act.dma_start(b2_sb[:, :], b2).then_inc(misc_in, 16)
            act.wait_ge(qk_psum, 1)
            nc.scalar.mul(qk0[:, :], bank[6][0:C0, 256:257 + MODEL], float(MODEL) ** -0.5).then_inc(qk_sb, 1)
            nc.scalar.mul(qk1[:, :], bank[7][0:C1 + 1, 256:257 + MODEL], float(MODEL) ** -0.5).then_inc(qk_sb, 1)
            for n, (rows, col, k) in enumerate(((LEVEL_TOKENS[2], EMBED, 1), (LEVEL_TOKENS[1], 0, 0))):
                act.wait_ge(tok_psum, n + 1)
                for b in range(BATCH):
                    nc.scalar.copy(t12[0:rows, k, EMBED * b:EMBED * (b + 1)],
                                   bank[2 + b][0:rows, col:col + EMBED]).then_inc(tok_sb, 1)
            act.wait_ge(wf_in, 16 * 3)
            for level in (2, 1):
                act.wait_ge(cat_psum, 3 - level)
                nc.scalar.activation(cat[:, level, :], bank[5 + level][:, 0:SEQ], ACT.Identity,
                                     bias=ebias[:, level:level + 1]).then_inc(cat_sb, 1)
            act.wait_ge(cat_psum, 3)
            for b in range(BATCH):
                r = slice(B1 * b, B1 * b + EMBED)
                nc.scalar.activation(cat[r, 0, :], bank[4 + b][r, 0:SEQ], ACT.Identity,
                                     bias=ebias[r, 0:1]).then_inc(cat_sb, 1)
            act.wait_ge(zt_psum, 1)
            nc.scalar.copy(zt0[:, 0:SEQ], bank[2][:, 0:SEQ])
            nc.scalar.copy(zt1[0:C1, 0:SEQ], bank[2][0:C1, SEQ:2 * SEQ]).then_inc(zt_sb, 1)
            act.wait_ge(q_psum, 1)
            nc.scalar.copy(qt0[:, :], bank[6][:, :]).then_inc(q_sb, 1)
            act.wait_ge(v_psum, 1)
            nc.scalar.copy(v_sb[:, 0:2, :], bank[4][:, 0:2 * MODEL]).then_inc(v_ready, 1)
            for t in range(TOKEN_TILES):
                act.wait_ge(nmax_ready, t // 2 + 1)
                nc.scalar.activation(probs[:, t, :], bank[t // 2][:, SEQ * (t % 2):SEQ * (t % 2 + 1)], ACT.Exp,
                                     bias=nmax[:, t:t + 1], accum_out=esum[:, t:t + 1]).then_inc(probs_ready, 1)
            act.wait_ge(pt_psum, 2)
            nc.scalar.copy(probs_t[:, 2:4, :, :], bank[3][:, :]).then_inc(pt_sb, 1)
            act.wait_ge(z2t_psum, 1)
            nc.scalar.copy(z2t0[:, 0:SEQ], bank[6][:, 0:SEQ])
            nc.scalar.copy(z2t1[:, 0:SEQ], bank[6][0:C1, SEQ:2 * SEQ]).then_inc(z2t_sb, 1)
            act.wait_ge(gap_ready, 1)
            nc.scalar.activation(egap[:, :], gap[:, :], ACT.Exp).then_inc(egap_ready, 1)
            act.wait_ge(comb_psum, 1)
            nc.scalar.copy(comb_t[:, :], bank[1][0:EXPERTS, :]).then_inc(comb_sb, 1)

            def gelu(par, products):
                for n in range(2):
                    act.wait_ge(up_psum, products + n + 1)
                    last = nc.scalar.activation(hid[:, n * NH:(n + 1) * NH], bank[2 * par + n][:, 0:NH], ACT.Gelu)
                last.then_inc(gelu_done, 1)

            gelu(0, 0)
            act.wait_ge(expert_ready, 1)
            used = act.value_load(tiles_used[0:1, 0:1], min_val=2, max_val=SLOT_TILES)
            with act.Fori(0, (SLOT_TILES + 1) // 2) as i:
                for par in range(2):
                    j = 2 * i + par
                    with act.If(j < used):
                        act.wait_ge(ht_psum, j + 1)
                        nc.scalar.copy(hid_t[:, 0:FK // 2, :], bank[4][:, 0:NH]).then_inc(ht_act, 1)
                        with act.If(j + 1 < used):
                            gelu(1 - par, 2 * j + 2)
                        act.nop()

        @block.vector
        def _(dve):
            chain = [0]

            def link(ins):
                chain[0] += 1
                ins.then_inc(dv, 1)
                dve.wait_ge(dv, chain[0])

            nc.vector.memset(ones_b[:, :], 1.0).then_inc(ones_ready, 1)
            nc.vector.memset(zt1[C1:C1 + 1, :], 1.0).then_inc(gp_set, 1)
            nc.vector.memset(xs1[0][C1:C1 + 1, :], 1.0).then_inc(gp_set, 1)
            nc.vector.memset(xs1[1][C1:C1 + 1, :], 1.0).then_inc(gp_set, 1)
            nc.vector.memset(ones8[:, :], 1.0).then_inc(gp_set, 1)
            link(nc.vector.memset(xtab[:, :, GATHER_ROWS:B1], 0.0))
            dve.wait_ge(x_in, 32)
            link(nc.vector.tensor_copy(xtab_hi[:, :, :], xtab[:, :, :]))
            nc.vector.tensor_tensor(xtab_lo[:, :, :], xtab[:, :, :], xtab_hi[:, :, :].bitcast(F),
                                    ALU.subtract).then_inc(xtab_ready, 1)
            dve.wait_ge(k_in, 16)

            def make_onehot(n):
                level, col, width, piece = pieces[n]
                dve.wait_ge(pick_in[piece], 16)
                if n >= 2:
                    dve.wait_ge(picked_psum, n - 1)
                for k in range(2):
                    nc.vector.tensor_scalar(onehot[:, n % 2, k, 0:width], pick_bytes[:, col:col + width, 0],
                                            K[:, K_LOW + k:K_LOW + k + 1], None,
                                            ALU.is_equal).then_inc(onehot_ready, 1)

            def mask_high(n):
                level, col, width, piece = pieces[n]
                dve.wait_ge(picked_psum, n + 1)
                nc.vector.scalar_tensor_tensor(
                    out=gathered[0:ROWS, col:col + width], in0=pick_bytes[0:ROWS, col:col + width, 1],
                    scalar=K[0:ROWS, K_HIGH + level:K_HIGH + level + 1], in1=bank[n % 2][0:ROWS, 0:width],
                    op0=ALU.is_equal, op1=ALU.mult).then_inc(picked_sb, 1)

            make_onehot(0)
            for n in range(1, len(pieces)):
                make_onehot(n)
                mask_high(n - 1)
            mask_high(len(pieces) - 1)

            def layer_norm(src, ready, rstd_done, dst, done):
                for t in range(TOKEN_TILES):
                    last = nc.vector.bn_stats(stats[:, t, :], src[:, t, :])
                link(last)
                for t in range(TOKEN_TILES):
                    last = nc.vector.bn_aggr(mv[:, t, :], stats[:, t, :])
                link(last)
                nc.vector.tensor_scalar(vareps[:, :], mv[:, :, 1], EPS, None, ALU.add).then_inc(ready, 1)
                dve.wait_ge(rstd_done, 1)
                for t in range(TOKEN_TILES):
                    nc.vector.tensor_scalar(dst[:, t, :], src[:, t, :], mv[:, t, 0:1], rstd[:, t:t + 1],
                                            ALU.subtract, ALU.mult).then_inc(done, 1)

            dve.wait_ge(wf_in, 16 * 3)
            for b in range(BATCH):
                dve.wait_ge(h_psum, b + 1)
                last = nc.vector.tensor_tensor(
                    h[:, 2 * b:2 * b + 2, :], bank[b][:, 0:2 * MODEL].rearrange("p (t c) -> p t c", t=2),
                    bf_sb[:, None, :].to_broadcast([P, 2, MODEL]), ALU.add)
            link(last)
            layer_norm(h, var_ready, rstd_ready, z, z_ready)
            dve.wait_ge(gp_set, 5)
            dve.wait_ge(zt_psum, 2)
            nc.vector.tensor_copy(zt0[:, SEQ:2 * SEQ], bank[3][:, 0:SEQ])
            nc.vector.tensor_copy(zt1[0:C1, SEQ:2 * SEQ], bank[3][0:C1, SEQ:2 * SEQ]).then_inc(zt_sb, 1)
            dve.wait_ge(q_psum, 2)
            nc.vector.tensor_copy(qt1[:, :], bank[7][0:C1 + 1, :]).then_inc(q_sb, 1)
            dve.wait_ge(v_psum, 2)
            nc.vector.tensor_copy(v_sb[:, 2:4, :], bank[5][:, 0:2 * MODEL]).then_inc(v_ready, 1)
            for b in range(BATCH):
                dve.wait_ge(score_psum, b + 1)
                nc.vector.tensor_reduce(nmax[:, 2 * b:2 * b + 2],
                                        bank[b][:, :].rearrange("p (t k) -> p t k", t=2),
                                        AX.X, ALU.max, negate=True).then_inc(nmax_ready, 1)
            dve.wait_ge(pt_psum, 1)
            nc.vector.tensor_copy(probs_t[:, 0:2, :, :], bank[2][:, :]).then_inc(pt_sb, 1)
            dve.wait_ge(probs_ready, TOKEN_TILES)
            link(nc.vector.reciprocal(rsum[:, :], esum[:, :]))
            for t in range(TOKEN_TILES):
                dve.wait_ge(pv_psum, t // 2 + 1)
                last = nc.vector.scalar_tensor_tensor(
                    out=h2[:, t, :], in0=bank[4 + t // 2][:, MODEL * (t % 2):MODEL * (t % 2 + 1)],
                    scalar=rsum[:, t:t + 1], in1=h[:, t, :], op0=ALU.mult, op1=ALU.add)
            link(last)
            layer_norm(h2, var2_ready, rstd2_ready, z2, z2_ready)
            dve.wait_ge(z2t_psum, 2)
            nc.vector.tensor_copy(z2t0[:, SEQ:2 * SEQ], bank[7][:, 0:SEQ])
            nc.vector.tensor_copy(z2t1[:, SEQ:2 * SEQ], bank[7][0:C1, SEQ:2 * SEQ]).then_inc(z2t_sb, 1)

            dve.wait_ge(logit_psum, 1)
            link(nc.vector.tensor_copy(logits[:, :, :], bank[0][:, 0:TOKEN_TILES * EXPERTS]))
            for t in range(TOKEN_TILES):
                last = nc.vector.max(top[:, t, :], logits[:, t, :])
            link(last)
            nc.vector.tensor_tensor(gap[:, :], top[:, :, 1], top[:, :, 0], ALU.subtract).then_inc(gap_ready, 1)
            for t in range(TOKEN_TILES):
                last = nc.vector.max_index(topi[:, t, :], top[:, t, :], logits[:, t, :])
            link(last)
            link(nc.vector.tensor_copy(topf[:, :, :], topi[:, :, 0:2].rearrange("p t c -> p c t")))
            for c in range(2):
                last = nc.vector.tensor_tensor(
                    chosen[:, c, :, :], iota[:, None, 0:EXPERTS].to_broadcast([P, TOKEN_TILES, EXPERTS]),
                    topf[:, c, :, None].to_broadcast([P, TOKEN_TILES, EXPERTS]), ALU.is_equal)
            link(last)
            nc.vector.tensor_tensor(member[:, :, :], chosen[:, 0, :, :], chosen[:, 1, :, :],
                                    ALU.add).then_inc(member_ready, 1)
            dve.wait_ge(egap_ready, 1)
            link(nc.vector.tensor_scalar(eden[:, :], egap[:, :], 1.0, None, ALU.add))
            link(nc.vector.reciprocal(wgt[:, 0, :], eden[:, :]))
            link(nc.vector.tensor_tensor(wgt[:, 1, :], egap[:, :], wgt[:, 0, :], ALU.mult))
            for c, dst in ((0, comb), (1, comb2)):
                last = nc.vector.tensor_tensor(dst[:, :, :], chosen[:, c, :, :],
                                               wgt[:, c, :, None].to_broadcast([P, TOKEN_TILES, EXPERTS]), ALU.mult)
            link(last)
            nc.vector.tensor_tensor(comb[:, :, :], comb[:, :, :], comb2[:, :, :], ALU.add).then_inc(comb_ready, 1)
            for c in range(2):
                nc.vector.tensor_copy(values[:, 4 * c:4 * c + 4, 0], K[:, K_TOKEN:K_TOKEN + TOKEN_TILES])
            wgt8 = wgt[:, :, :].rearrange("p c t -> p (c t)")
            link(nc.vector.tensor_copy(wgt_hi[:, :], wgt8))
            nc.vector.tensor_copy(values[:, :, 1], wgt_hi[:, :].bitcast(F))
            link(nc.vector.tensor_tensor(values[:, :, 2], wgt8, wgt_hi[:, :].bitcast(F), ALU.subtract))
            dve.wait_ge(rank_psum, 1)
            link(nc.vector.tensor_scalar(cnti[:, :], bank[4][:, 32:32 + EXPERTS], float(P - 1), None, ALU.add))
            link(nc.vector.tensor_single_scalar(ntile[:, :], cnti[:, :], 7, ALU.logical_shift_right))
            link(nc.vector.tensor_tensor_scan(tile_end[:, :], ones8[:, :], ntile[:, :], 0.0, ALU.mult, ALU.add))
            link(nc.vector.tensor_tensor(base[:, :], tile_end[:, :], ntile[:, :], ALU.subtract))
            link(nc.vector.scalar_tensor_tensor(
                out=slot[:, :, :], in0=base[:, None, :].to_broadcast([P, TOKEN_TILES, EXPERTS]), scalar=float(P),
                in1=bank[4][:, 0:32].rearrange("p (t e) -> p t e", t=TOKEN_TILES), op0=ALU.mult, op1=ALU.add))
            link(nc.vector.tensor_tensor(picked[:, :, :, :], chosen[:, :, :, :],
                                         slot[:, None, :, :].to_broadcast([P, 2, TOKEN_TILES, EXPERTS]), ALU.mult))
            link(nc.vector.tensor_reduce(slotf[:, :], picked[:, :, :, :].rearrange("p c t e -> p (c t) e"),
                                         AX.X, ALU.add))
            link(nc.vector.tensor_copy(sloti[:, :], slotf[:, :]))
            nc.vector.tensor_single_scalar(slot_tile[:, :], sloti[:, :], 7, ALU.logical_shift_right)
            link(nc.vector.tensor_single_scalar(slot_row[:, :], sloti[:, :], P - 1, ALU.bitwise_and))
            link(nc.vector.tensor_tensor(in_tile[:, :, :], iota[:, None, 0:TABLE].to_broadcast([P, 8, TABLE]),
                                         slot_tile[:, :, None].to_broadcast([P, 8, TABLE]), ALU.is_equal))
            nc.vector.tensor_tensor(
                payload[:, :, :, :], in_tile[:, :, None, :].to_broadcast([P, 8, 3, TABLE]),
                values[:, :, :, None].to_broadcast([P, 8, 3, TABLE]), ALU.mult)
            nc.vector.tensor_tensor(in_row[:, :, :], iota[:, None, :].to_broadcast([P, 8, P]),
                                    slot_row[:, :, None].to_broadcast([P, 8, P]), ALU.is_equal).then_inc(payload_ready, 1)
            link(nc.vector.tensor_tensor(before[:, :, :], tile_end[:, None, :].to_broadcast([P, TABLE, EXPERTS]),
                                         iota[:, 0:TABLE, None].to_broadcast([P, TABLE, EXPERTS]), ALU.is_le))
            link(nc.vector.tensor_reduce(expertf[:, :], before[:, :, :], AX.X, ALU.add))
            nc.vector.tensor_scalar(expert[:, :], expertf[:, :], float(EXPERTS - 1), None, ALU.min)
            nc.vector.tensor_copy(tiles_used[:, :], tile_end[:, EXPERTS - 1:EXPERTS]).then_inc(expert_ready, 1)
            dve.wait_ge(table_psum, 1)
            token_psum = bank[5][:, 0:TABLE]
            nc.vector.tensor_scalar(gidx[:, :], token_psum, 1.0, 0.0, ALU.subtract, ALU.max).then_inc(gidx_ready, 1)
            link(nc.vector.tensor_copy(table[:, :, :], bank[5][:, 0:3 * TABLE]))
            nc.vector.tensor_tensor(slot_w[:, :], table[:, 1, :], table[:, 2, :], ALU.add)
            link(nc.vector.tensor_scalar(pad[:, :], table[:, 0, :], 0.0, 8192.0, ALU.is_equal, ALU.mult))
            link(nc.vector.tensor_tensor(sidxf[:, :], table[:, 0, :], pad[:, :], ALU.add))
            nc.vector.tensor_scalar(sidx[:, :], sidxf[:, :], 1.0, None, ALU.subtract).then_inc(table_ready, 1)

            def copy_rows(par):
                nc.vector.tensor_copy(xs0[par][:, :], bank[6][:, 0:P])
                nc.vector.tensor_copy(xs1[par][0:C1, :], bank[6][0:C1, P:2 * P]).then_inc(xt_copied, 1)

            for b in range(BATCH):
                dve.wait_ge(init_psum, b + 1)
                nc.vector.tensor_tensor(out_init[:, 2 * b:2 * b + 2, :],
                                        bank[2 + b][:, 0:2 * MODEL].rearrange("p (t c) -> p t c", t=2),
                                        h2[:, 2 * b:2 * b + 2, :], ALU.add).then_inc(init_sb, 1)
            for j in range(2):
                dve.wait_ge(xt_psum, j + 1)
                copy_rows(j)
            dve.sem_inc(y_free, 1)
            used = dve.value_load(tiles_used[0:1, 0:1], min_val=2, max_val=SLOT_TILES)
            with dve.Fori(0, (SLOT_TILES + 1) // 2) as i:
                for par in range(2):
                    j = 2 * i + par
                    with dve.If(j < used):
                        dve.wait_ge(ht_psum, j + 1)
                        nc.vector.tensor_copy(hid_t[:, FK // 2:FK, :], bank[5][:, 0:NH]).then_inc(ht_dve, 1)
                        with dve.If(j + 1 < used):
                            dve.wait_ge(xt_psum, j + 3)
                            copy_rows(par)
                        dve.wait_ge(ys_free, j + 1)
                        dve.wait_ge(y_psum, j + 1)
                        nc.vector.tensor_scalar(ys[par][:, :], bank[7][:, 0:MODEL], slot_w[:, bass.ds(j, 1)], None,
                                                ALU.mult).then_inc(y_ready, 1)
                        dve.wait_ge(y_ready, j + 1)
                        dve.sem_inc(y_free, 1)

        @block.tensor
        def _(pe):
            def keep_warm(n, bank_n):
                for _ in range(n):
                    nc.tensor.matmul(bank[bank_n][:, :], ones_b[:, 0:P], ones_b[:, :], start=True, stop=True)

            pe.wait_ge(ones_ready, 1)
            keep_warm(17, 0)
            pe.wait_ge(attn_in, 16 * 2)
            for bank_n, cols in ((6, slice(0, C0)), (7, slice(C0, MODEL + 1))):
                m = cols.stop - cols.start
                for (lhs, rhs), first in (((wq0, wk0), True), ((wq1, wk1), False)):
                    last = nc.tensor.matmul(bank[bank_n][0:m, 256:257 + MODEL], lhs[:, cols], rhs[:, :],
                                            start=first, stop=not first)
            last.then_inc(qk_psum, 1)
            pe.wait_ge(xtab_ready, 1)

            def pick(n):
                level, col, width, piece = pieces[n]
                if n >= 2:
                    pe.wait_ge(picked_sb, n - 1)
                for k in range(2):
                    pe.wait_ge(onehot_ready, 2 * n + k + 1)
                    for part, tab in enumerate((xtab_hi, xtab_lo)):
                        last = nc.tensor.matmul(bank[n % 2][0:ROWS, 0:width], tab[:, 2 * level + k, :],
                                                onehot[:, n % 2, k, 0:width],
                                                start=(k == 0 and part == 0), stop=(k == 1 and part == 1))
                last.then_inc(picked_psum, 1)

            def small_level(level, col):
                nt = LEVEL_TOKENS[level]
                for g in range(GROUP):
                    for b in range(BATCH):
                        r = slice(B1 * b, B1 * b + GATHER_ROWS)
                        c = START[level] + g * nt
                        last = nc.tensor.matmul(bank[2 + b][0:nt, col:col + EMBED], gathered[r, c:c + nt],
                                                we_sb[r, level, g, :], start=(g == 0), stop=(g == GROUP - 1))
                last.then_inc(tok_psum, 1)

            def fine_level(groups):
                for g in groups:
                    for b in range(BATCH):
                        r = slice(B1 * b, B1 * b + GATHER_ROWS)
                        c = START[0] + g * SEQ
                        last = nc.tensor.matmul(bank[4 + b][B1 * b:B1 * b + EMBED, 0:SEQ], we_sb[r, 0, g, :],
                                                gathered[r, c:c + SEQ], start=(g == 0), stop=(g == GROUP - 1))
                return last

            pick(0)
            pick(1)
            pe.wait_ge(we_in[2], 32)
            pe.wait_ge(picked_sb, 1)
            small_level(2, EMBED)
            pick(2)
            pick(3)
            pe.wait_ge(picked_sb, 3)
            pe.wait_ge(we_in[1], 32)
            pe.wait_ge(tok_sb, 2)
            small_level(1, 0)
            pe.wait_ge(kmat_in, 16)
            pe.wait_ge(qk_sb, 2)
            pe.wait_ge(tok_sb, 2)
            nc.tensor.matmul(bank[7][:, 0:SEQ], t12[0:LEVEL_TOKENS[2], 1, :],
                             K[0:LEVEL_TOKENS[2], K_UP2:K_UP2 + SEQ], start=True, stop=True).then_inc(cat_psum, 1)
            pe.wait_ge(tok_sb, 4)
            nc.tensor.matmul(bank[6][:, 0:SEQ], t12[0:LEVEL_TOKENS[1], 0, :],
                             K[0:LEVEL_TOKENS[1], K_UP1:K_UP1 + SEQ], start=True, stop=True).then_inc(cat_psum, 1)
            pe.wait_ge(we_in[0], 32)
            keep_warm(6, 2)
            for n in range(4, len(pieces)):
                pick(n)
                pe.wait_ge(picked_sb, n)
                last = fine_level(range(2 * (n - 4), 2 * (n - 3)))
            pe.wait_ge(picked_sb, len(pieces))
            fine_level(range(2 * (len(pieces) - 4), GROUP)).then_inc(cat_psum, 1)
            keep_warm(3, 2)
            pe.wait_ge(wf_in, 16 * 3)
            pe.wait_ge(cat_sb, 4)
            for b in range(BATCH):
                r = slice(B1 * b, B1 * b + EMBED)
                for half in range(2):
                    for level in range(LEVELS):
                        last = nc.tensor.matmul(bank[b][:, MODEL * half:MODEL * (half + 1)],
                                                cat[r, level, P * half:P * (half + 1)], wf_sb[r, level, :],
                                                start=(level == 0), stop=(level == LEVELS - 1))
                last.then_inc(h_psum, 1)

            def transposes(src, done, bank0, signal):
                for b in range(BATCH):
                    for half in range(2):
                        t = 2 * b + half
                        pe.wait_ge(done, t + 1)
                        c = P * half
                        nc.tensor.transpose(bank[bank0 + b][:, c:c + P], src[:, t, 0:C0], ident)
                        last = nc.tensor.transpose(bank[bank0 + b][0:C1, SEQ + c:SEQ + c + P], src[:, t, C0:MODEL],
                                                   ident)
                    last.then_inc(signal, 1)

            keep_warm(9, 6)
            transposes(z, z_ready, 2, zt_psum)
            pe.wait_ge(zt_sb, 2)
            for n, (bank_n, cols) in enumerate(((6, slice(0, C0)), (7, slice(C0, MODEL + 1)))):
                m = cols.stop - cols.start
                nc.tensor.matmul(bank[bank_n][0:m, :], qk0[:, cols], zt0[:, :], start=True, stop=False)
                nc.tensor.matmul(bank[bank_n][0:m, :], qk1[:, cols], zt1[:, :], start=False,
                                 stop=True).then_inc(q_psum, 1)
            for t in range(TOKEN_TILES):
                o = bank[4 + t // 2][:, MODEL * (t % 2):MODEL * (t % 2 + 1)]
                nc.tensor.matmul(o, zt0[:, P * t:P * (t + 1)], wv0[:, :], start=True, stop=False)
                last = nc.tensor.matmul(o, zt1[:, P * t:P * (t + 1)], wv1[:, :], start=False, stop=True)
                if t % 2:
                    last.then_inc(v_psum, 1)
            pe.wait_ge(q_sb, 2)
            for t in range(TOKEN_TILES):
                b = t // 2
                o = bank[b][:, SEQ * (t % 2):SEQ * (t % 2 + 1)]
                nc.tensor.matmul(o, qt0[:, P * t:P * (t + 1)], zt0[:, SEQ * b:SEQ * (b + 1)], start=True, stop=False)
                last = nc.tensor.matmul(o, qt1[:, P * t:P * (t + 1)], zt1[:, SEQ * b:SEQ * (b + 1)],
                                        start=False, stop=True)
                if t % 2:
                    last.then_inc(score_psum, 1)
            keep_warm(6, 6)
            for t in range(TOKEN_TILES):
                pe.wait_ge(probs_ready, t + 1)
                for k in range(2):
                    c = P * (2 * (t % 2) + k)
                    last = nc.tensor.transpose(bank[2 + t // 2][:, c:c + P], probs[:, t, P * k:P * (k + 1)], ident)
                if t % 2:
                    last.then_inc(pt_psum, 1)
            pe.wait_ge(v_ready, 2)
            pe.wait_ge(pt_sb, 2)
            for t in range(TOKEN_TILES):
                o = bank[4 + t // 2][:, MODEL * (t % 2):MODEL * (t % 2 + 1)]
                for k in range(2):
                    last = nc.tensor.matmul(o, probs_t[:, t, k, :], v_sb[:, 2 * (t // 2) + k, :],
                                            start=(k == 0), stop=(k == 1))
                if t % 2:
                    last.then_inc(pv_psum, 1)
            keep_warm(10, 2)
            transposes(z2, z2_ready, 6, z2t_psum)
            pe.wait_ge(z2t_sb, 2)
            pe.wait_ge(misc_in, 16)
            for t in range(TOKEN_TILES):
                o = bank[0][:, EXPERTS * t:EXPERTS * (t + 1)]
                nc.tensor.matmul(o, z2t0[:, P * t:P * (t + 1)], rw0[:, :], start=True, stop=False)
                last = nc.tensor.matmul(o, z2t1[:, P * t:P * (t + 1)], rw1[:, :], start=False, stop=True)
            last.then_inc(logit_psum, 1)
            pe.wait_ge(gp_set, 5)
            keep_warm(4, 2)
            pe.wait_ge(member_ready, 1)
            memb = member[:, :, :].rearrange("p t e -> p (t e)")
            nc.tensor.matmul(bank[4][:, 0:32], tri_b[:, :], memb, start=True, stop=False, skip_group_check=True)
            for t in range(1, TOKEN_TILES):
                nc.tensor.matmul(bank[4][:, EXPERTS * t:32], ones_b[:, 0:P], memb[:, 0:32 - EXPERTS * t],
                                 start=False, stop=False, skip_group_check=True)
            for t in range(TOKEN_TILES):
                last = nc.tensor.matmul(bank[4][:, 32:32 + EXPERTS], ones_b[:, 0:P],
                                        memb[:, EXPERTS * t:EXPERTS * (t + 1)],
                                        start=False, stop=(t == TOKEN_TILES - 1), skip_group_check=True)
            last.then_inc(rank_psum, 1)
            pe.wait_ge(comb_ready, 1)
            for t in range(TOKEN_TILES):
                last = nc.tensor.transpose(bank[1][0:EXPERTS, P * t:P * (t + 1)], comb[:, t, :], ident)
            last.then_inc(comb_psum, 1)
            keep_warm(8, 7)
            pe.wait_ge(payload_ready, 1)
            for c in range(2 * TOKEN_TILES):
                last = nc.tensor.matmul(bank[5][:, 0:3 * TABLE], in_row[:, c, :],
                                        payload[:, c, :, :].rearrange("p v t -> p (v t)"),
                                        start=(c == 0), stop=(c == 2 * TOKEN_TILES - 1))
            last.then_inc(table_psum, 1)
            pe.wait_ge(comb_sb, 1)
            for t in range(TOKEN_TILES):
                last = nc.tensor.matmul(bank[2 + t // 2][:, MODEL * (t % 2):MODEL * (t % 2 + 1)],
                                        comb_t[:, P * t:P * (t + 1)], b2_sb[:, :], start=True, stop=True)
                if t % 2:
                    last.then_inc(init_psum, 1)

            def transpose_rows(par):
                nc.tensor.transpose(bank[6][:, 0:P], xg[par][:, 0:C0], ident)
                nc.tensor.transpose(bank[6][0:C1, P:2 * P], xg[par][:, C0:MODEL], ident).then_inc(xt_psum, 1)

            def up(e, par, n):
                at = e * HIDDEN + n * NH
                nc.tensor.matmul(bank[2 * par + n][:, 0:NH], xs0[par][:, :], w1_0[:, bass.ds(at, NH)],
                                 start=True, stop=False)
                nc.tensor.matmul(bank[2 * par + n][:, 0:NH], xs1[par][:, :], w1_1[:, bass.ds(at, NH)],
                                 start=False, stop=True).then_inc(up_psum, 1)

            expert_of = [pe.alloc_register(f"expert_of_{par}") for par in range(2)]

            def expert_value(par):
                return pe.snap(expert_of[par], min_val=0, max_val=EXPERTS - 1)

            def transpose_hidden():
                for k in range(FK):
                    c = P * (k % 3)
                    last = nc.tensor.transpose(bank[4 + k // 3][:, c:c + P], hid[:, k * P:(k + 1) * P], ident)
                last.then_inc(ht_psum, 1)

            pe.wait_ge(gather_done[0], 16)
            transpose_rows(0)
            pe.wait_ge(init_sb, 2)
            pe.wait_ge(expert_ready, 1)
            pe.wait_ge(moe_in, 16 * (3 * EXPERTS // 2 + 1))
            used = pe.value_load(tiles_used[0:1, 0:1], min_val=2, max_val=SLOT_TILES)
            for par in range(2):
                pe.reg_load(expert_of[par], expert[0:1, par:par + 1])
            pe.wait_ge(xt_copied, 1)
            first = expert_value(0)
            up(first, 0, 0)
            pe.wait_ge(gather_done[1], 16)
            transpose_rows(1)
            up(first, 0, 1)
            with pe.Fori(0, (SLOT_TILES + 1) // 2) as i:
                for par in range(2):
                    j, other = 2 * i + par, 1 - par
                    with pe.If(j < used):
                        with pe.If(j + 1 < used):
                            pe.wait_ge(xt_copied, j + 2)
                            nxt = expert_value(other)
                            up(nxt, other, 0)
                            pe.wait_ge(gather_done[par], 16 * i + 32)
                            pe.wait_ge(gelu_done, j + 1)
                            transpose_hidden()
                            transpose_rows(par)
                            up(nxt, other, 1)
                        with pe.Else():
                            pe.wait_ge(gelu_done, j + 1)
                            transpose_hidden()
                        own = expert_value(par)
                        pe.reg_load(expert_of[par], expert[0:1, bass.ds(j + 2, 1)])
                        pe.wait_ge(y_free, j + 1)
                        pe.wait_ge(ht_act, j + 1)
                        pe.wait_ge(ht_dve, j + 1)
                        for k in range(FK):
                            last = nc.tensor.matmul(bank[7][:, 0:MODEL], hid_t[:, k, :],
                                                    w2_sb[:, bass.ds(own * (FK * MODEL) + k * MODEL, MODEL)],
                                                    start=(k == 0), stop=(k == FK - 1))
                        last.then_inc(y_psum, 1)


def kernel(**inputs):
    import concourse.bacc as bacc
    from concourse.bass_utils import run_bass_kernel_spmd

    a = {k: np.asarray(v) for k, v in inputs.items()}
    x = a["x"]

    tables = []
    for level, p in enumerate((1, 2, 4)):
        side = IMAGE // p
        t = x.reshape(BATCH, CHANNELS, side, p, side, p).transpose(2, 4, 0, 3, 5, 1)
        t = t.reshape(PATCHES[level] // LOW, 2, P, BATCH, FEATURES[level])
        tables.append(t.transpose(2, 1, 3, 0, 4).reshape(P, 2, 1, BATCH * GATHER_ROWS))
    xt = np.concatenate(tables, axis=2).transpose(0, 2, 1, 3).reshape(P, 2 * LEVELS, BATCH * GATHER_ROWS)
    idx = np.concatenate([a[f"L0_tok_idx{level}"].reshape(-1, GROUP).T.reshape(-1) for level in (2, 1, 0)])
    arrays = {"xt": xt, "idx": idx}
    for level in range(LEVELS):
        w = a[f"L0_tok_W{level}"].reshape(EMBED, GROUP, FEATURES[level])
        arrays[f"we{level}"] = w.transpose(2, 1, 0)
    wf = a["L0_tok_Wf"].T.reshape(LEVELS, EMBED, MODEL).transpose(1, 0, 2).reshape(EMBED, LEVELS * MODEL)
    arrays["fuse"] = np.concatenate([wf] + [a[f"L0_tok_b{level}"][:, None] for level in range(LEVELS)], axis=1)
    arrays["bf"] = a["L0_tok_bf"]
    attn = np.zeros((MODEL + 1, A_END), np.float32)
    for col, name in ((A_Q, "q"), (A_K, "k")):
        attn[:MODEL, col:col + MODEL], attn[:MODEL, col + MODEL] = a[f"L0_attn_W{name}"], a[f"L0_attn_b{name}"]
    attn[:MODEL, A_V:A_R], attn[MODEL, A_V:A_R] = a["L0_attn_Wv"].T, a["L0_attn_bv"]
    attn[:MODEL, A_R:] = a["L0_ffn_router_w"].T
    arrays["attn"] = attn
    arrays["w1"], arrays["b1"] = a["L0_ffn_w1"], a["L0_ffn_b1"].reshape(1, EXPERTS * HIDDEN)
    arrays["w2"], arrays["b2"] = a["L0_ffn_w2"], a["L0_ffn_b2"]

    k = np.zeros((P, K_END), np.float32)
    p = np.arange(P)
    k[:, K_IDENT:K_TRI] = np.eye(P)
    k[:, K_TRI:K_IOTA] = p[:, None] < p[None, :]
    k[:, K_IOTA:K_UP1] = p[None, :]
    for level, col in ((1, K_UP1), (2, K_UP2)):
        n = LEVEL_TOKENS[level]
        pos = np.clip((np.arange(SEQ, dtype=np.float32) + 0.5) * (n / SEQ) - 0.5, 0.0, n - 1)
        lo = np.floor(pos).astype(int)
        hi = np.minimum(lo + 1, n - 1)
        up = np.zeros((n, SEQ), np.float32)
        np.add.at(up, (lo, np.arange(SEQ)), 1.0 - (pos - lo))
        np.add.at(up, (hi, np.arange(SEQ)), pos - lo)
        k[:n, col:col + SEQ] = up
    k[:, K_LOW], k[:, K_LOW + 1] = p, p + P
    for level in range(LEVELS):
        k[:, K_HIGH + level] = (p % B1) // FEATURES[level]
    for t in range(TOKEN_TILES):
        k[:, K_TOKEN + t] = t * P + p + 1
    k[:, K_HALF:K_IDENT] = -0.5
    arrays["consts"] = k

    nc = bacc.Bacc("TRN2", target_bir_lowering=False, num_devices=1)
    aps, feeds = {}, {}
    for name, array in arrays.items():
        array = np.ascontiguousarray(array)
        feeds[f"in_{name}"] = array
        aps[name] = nc.dram_tensor(f"in_{name}", array.shape, mybir.dt.from_np(array.dtype), kind="ExternalInput").ap()
    out = nc.dram_tensor("out", (TOKENS, MODEL), mybir.dt.float32, kind="ExternalOutput").ap()
    build(nc, aps["xt"], aps["idx"], [aps[f"we{level}"] for level in range(LEVELS)], aps["fuse"], aps["bf"],
          aps["attn"], aps["w1"], aps["b1"], aps["w2"], aps["b2"], aps["consts"], out)
    result = run_bass_kernel_spmd(nc, [feeds], core_ids=[0])
    return result.results[0]["out"].reshape(BATCH, SEQ, MODEL)
```

```python
import numpy as np
import concourse.bass as bass
from concourse import mybir
from contextlib import ExitStack

BATCH, CHANNELS, IMAGE = 2, 3, 64
GROUP = 16
EMBED, LEVELS = 64, 3
MODEL = EMBED * LEVELS
EXPERTS, HIDDEN = 8, 768
SEQ = IMAGE * IMAGE // GROUP
TOKENS = BATCH * SEQ
PATCHES = [4096, 1024, 256]
LEVEL_TOKENS = [n // GROUP for n in PATCHES]
FEATURES = [3, 12, 48]
P = 128
LOW = 256
GATHER_ROWS = 48
B1 = 64
ROWS = B1 + GATHER_ROWS
PICKS = sum(PATCHES)
START = [PATCHES[1] + PATCHES[2], PATCHES[2], 0]
TOKEN_TILES = TOKENS // P
C0, C1 = P, MODEL - P
XG = MODEL + C1
SLOT_TILES = 2 * TOKENS // P + EXPERTS - 1
AHEAD = 4
TABLE = 2 * ((SLOT_TILES + AHEAD) // 2 + 1)
FK = HIDDEN // P
NH = HIDDEN // 2
EPS = 1e-5

K_LOW = 0
K_HIGH = K_LOW + 2
K_TOKEN = K_HIGH + LEVELS
K_HALF = K_TOKEN + TOKEN_TILES
K_ROW = K_HALF + TOKEN_TILES
K_LOWER = K_ROW + 1
K_SIGN = K_LOWER + 1
K_IDENT = K_SIGN + 2
K_TRI = K_IDENT + P
K_IOTA = K_TRI + P
K_UP1 = K_IOTA + P
K_UP2 = K_UP1 + SEQ
K_END = K_UP2 + SEQ
A_Q, A_K, A_V, A_R = 0, MODEL + 1, 2 * (MODEL + 1), 3 * MODEL + 2
A_END = A_R + EXPERTS


def build(nc, xt, idx, we, fuse, bf, attn, w1, b1, w2, b2, consts, out):
    F, R, I32, U32, U8, BF = (mybir.dt.float32, mybir.dt.float32r, mybir.dt.int32, mybir.dt.uint32,
                              mybir.dt.uint8, mybir.dt.bfloat16)
    ALU, ACT, AX = mybir.AluOpType, mybir.ActivationFunctionType, mybir.AxisListType
    ctx = ExitStack()
    with ctx:
        def sb(name, shape, dt=F):
            return ctx.enter_context(nc.sbuf_tensor(name, shape, dt))

        def sem(name):
            return ctx.enter_context(nc.semaphore(name))

        z2_dram = nc.dram_tensor("z2_dram", (TOKENS, XG), F).ap()

        K = sb("K", [P, K_END])
        ident, tri, iota = K[:, K_IDENT:K_TRI], K[:, K_TRI:K_IOTA], K[:, K_IOTA:K_UP1]
        picks = sb("picks", [P, PICKS], I32)
        pick_bytes = picks[:, :].bitcast(U8).rearrange("p (j f) -> p j f", f=4)
        old_picks = picks[:, :].bitcast(F)

        def cut(space, start, *dims):
            view = space[:, start:start + int(np.prod(dims))]
            names = " ".join("abc"[:len(dims)])
            return view.rearrange(f"p ({names}) -> p {names}", **dict(zip("abc", dims))) if len(dims) > 1 else view

        probs = cut(old_picks, 0, TOKEN_TILES, SEQ)
        probs_t = cut(old_picks, 1024, TOKEN_TILES, 2, P)
        qt0 = cut(old_picks, 2048, TOKENS)
        qt1 = cut(old_picks, 2560, TOKENS)[0:C1 + 1]
        v_sb = cut(old_picks, 3072, TOKEN_TILES, MODEL)
        out_init = cut(old_picks, 3840, TOKEN_TILES, MODEL)
        fuse_sb = sb("fuse_sb", [P, LEVELS * (MODEL + 1)])
        wf_sb = fuse_sb[:, 0:LEVELS * MODEL].rearrange("p (l c) -> p l c", l=LEVELS)
        ebias = fuse_sb[:, LEVELS * MODEL:LEVELS * (MODEL + 1)]
        t12 = sb("t12", [P, 2, EMBED])
        cat = sb("cat", [P, LEVELS, SEQ])
        bf_sb = sb("bf_sb", [P, MODEL])
        attn0, attn1 = sb("attn0", [C0, A_END]), sb("attn1", [C1 + 1, A_END])
        wq0, wq1 = attn0[:, A_Q:A_K], attn1[0:C1, A_Q:A_K]
        wk0, wk1 = attn0[:, A_K:A_V], attn1[0:C1, A_K:A_V]
        wv0, wv1 = attn0[:, A_V:A_R], attn1[:, A_V:A_R]
        rw0, rw1 = attn0[:, A_R:A_END], attn1[0:C1, A_R:A_END]
        qk0, qk1 = sb("qk0", [C0, MODEL + 1]), sb("qk1", [C1 + 1, MODEL + 1])
        h = sb("h", [P, TOKEN_TILES, MODEL])
        stats = sb("stats", [P, TOKEN_TILES, 6])
        mv = sb("mv", [P, TOKEN_TILES, 2])
        vareps = sb("vareps", [P, TOKEN_TILES])
        rstd = sb("rstd", [P, TOKEN_TILES])
        z = sb("z", [P, TOKEN_TILES, MODEL])
        zt0, zt1 = sb("zt0", [C0, TOKENS]), sb("zt1", [C1 + 1, TOKENS])
        nmax = sb("nmax", [P, TOKEN_TILES])
        esum = sb("esum", [P, TOKEN_TILES])
        rsum = sb("rsum", [P, TOKEN_TILES])
        h2 = sb("h2", [P, TOKEN_TILES, MODEL])
        b2_sb = sb("b2_sb", [EXPERTS, MODEL])
        ones_b = sb("ones_b", [P, 512], BF)
        tri_b = sb("tri_b", [P, P], BF)
        ones8 = sb("ones8", [P, EXPERTS])
        logits = sb("logits", [P, TOKEN_TILES, EXPERTS])
        top = sb("top", [P, TOKEN_TILES, EXPERTS])
        topi = sb("topi", [P, TOKEN_TILES, EXPERTS], U32)
        gap = sb("gap", [P, TOKEN_TILES])
        egap = sb("egap", [P, TOKEN_TILES])
        eden = sb("eden", [P, TOKEN_TILES])
        wgt = sb("wgt", [P, 2, TOKEN_TILES])
        chosen = sb("chosen", [P, 2, TOKEN_TILES, EXPERTS])
        member = sb("member", [P, TOKEN_TILES, EXPERTS], BF)
        cnti = sb("cnti", [P, EXPERTS], I32)
        ntile = sb("ntile", [P, EXPERTS], I32)
        tile_end = sb("tile_end", [P, EXPERTS])
        base = sb("base", [P, EXPERTS])
        slot = sb("slot", [P, TOKEN_TILES, EXPERTS])
        picked = sb("picked", [P, 2, TOKEN_TILES, EXPERTS])
        slotf = sb("slotf", [P, 2 * TOKEN_TILES])
        sloti = sb("sloti", [P, 2 * TOKEN_TILES], I32)
        slot_tile = sb("slot_tile", [P, 2 * TOKEN_TILES], I32)
        slot_row = sb("slot_row", [P, 2 * TOKEN_TILES], I32)
        in_tile = sb("in_tile", [P, 2 * TOKEN_TILES, TABLE])
        payload = sb("payload", [P, 2 * TOKEN_TILES, 3, TABLE], R)
        values = sb("values", [P, 2 * TOKEN_TILES, 3])
        wgt_hi = sb("wgt_hi", [P, 2 * TOKEN_TILES], R)
        table = sb("table", [P, 3, TABLE])
        slot_w = sb("slot_w", [P, TABLE])
        gidx = sb("gidx", [P, TABLE], I32)
        pad = sb("pad", [P, TABLE])
        sidxf = sb("sidxf", [P, TABLE])
        sidx = sb("sidx", [P, TABLE], I32)
        before = sb("before", [P, TABLE, EXPERTS])
        expertf = sb("expertf", [P, TABLE])
        expert = sb("expert", [P, TABLE], I32)
        tiles_used = sb("tiles_used", [P, 1], I32)
        comb = sb("comb", [P, TOKEN_TILES, EXPERTS])
        comb2 = sb("comb2", [P, TOKEN_TILES, EXPERTS])
        comb_t = sb("comb_t", [EXPERTS, TOKENS])
        b1_raw, b1_rows = sb("b1_raw", [P, NH]), sb("b1_rows", [P, NH], R)
        is_expert = sb("is_expert", [P, TABLE])
        pick_b1 = [sb(f"pick_b1_{i}", [P, P], R) for i in range(2)]
        w2_sb = sb("w2_sb", [P, EXPERTS * FK * MODEL])
        gi_col = [sb(f"gi_col{i}", [P, 1], I32) for i in range(2)]
        si_col = [sb(f"si_col{i}", [P, 1], I32) for i in range(2)]
        xg = [sb(f"xg{i}", [P, XG]) for i in range(2)]
        x0_high = [sb(f"x0_high{i}", [C0, P], R) for i in range(2)]
        x0_low = [sb(f"x0_low{i}", [C0, P], R) for i in range(2)]
        x1_high = [sb(f"x1_high{i}", [P, P], R) for i in range(2)]
        x1_low = [sb(f"x1_low{i}", [P, P], R) for i in range(2)]
        ys = [sb(f"ys{i}", [P, MODEL]) for i in range(2)]

        with ExitStack() as raw:
            w1_0_raw = raw.enter_context(nc.sbuf_tensor("w1_0_raw", [C0, EXPERTS * HIDDEN], F))
            w1_1_raw = raw.enter_context(nc.sbuf_tensor("w1_1_raw", [P, EXPERTS * HIDDEN], F))
        w1_0_low = sb("w1_0_low", [C0, EXPERTS * HIDDEN], R)
        w1_1 = sb("w1_1", [P, EXPERTS * HIDDEN], R)
        with ExitStack() as front:
            def fsb(name, shape, dt=F):
                return front.enter_context(nc.sbuf_tensor(name, shape, dt))

            xtab = fsb("xtab", [P, 2 * LEVELS, ROWS])
            xtab_hi = fsb("xtab_hi", [P, 2 * LEVELS, ROWS], R)
            xtab_lo = fsb("xtab_lo", [P, 2 * LEVELS, ROWS], R)
            onehot = fsb("onehot", [P, 2, 2, 512], R)
            gathered = fsb("gathered", [P, PICKS])
            we_sb = fsb("we_sb", [P, LEVELS, GROUP, EMBED])
        w1_0_high = sb("w1_0_high", [C0, EXPERTS * HIDDEN], R)
        w1_1_high = sb("w1_1_high", [P, 3, HIDDEN], R)
        z2 = sb("z2", [P, TOKEN_TILES, MODEL])
        z2t0, z2t1 = sb("z2t0", [C0, TOKENS]), sb("z2t1", [C1, TOKENS])
        in_row = sb("in_row", [P, 2 * TOKEN_TILES, P], R)
        hid = sb("hid", [P, HIDDEN])
        hid_t = sb("hid_t", [P, FK, P])

        bank = [ctx.enter_context(nc.psum_tensor(f"bank{i}", [P, 512], F)) for i in range(8)]

        k_in, kmat_in, wf_in = sem("k_in"), sem("kmat_in"), sem("wf_in")
        x_in = [sem(f"x_in{level}") for level in range(LEVELS)]
        we_in = [sem(f"we_in{level}") for level in range(LEVELS)]
        attn_in, misc_in, w2_in = sem("attn_in"), sem("misc_in"), sem("w2_in")
        w1_in = [sem(f"w1_in{i}") for i in range(EXPERTS // 2)]
        pick_in = [sem(f"pick_in{i}") for i in range(7)]
        ones_ready, dv, gp_set = sem("ones_ready"), sem("dv"), sem("gp_set")
        xtab_ready, onehot_ready, picked_psum, picked_sb = (sem("xtab_ready"), sem("onehot_ready"),
                                                            sem("picked_psum"), sem("picked_sb"))
        tok_psum, tok_sb, cat_psum, cat_sb = sem("tok_psum"), sem("tok_sb"), sem("cat_psum"), sem("cat_sb")
        qk_psum, qk_sb = sem("qk_psum"), sem("qk_sb")
        h_psum, h_ready, var_ready, rstd_ready = sem("h_psum"), sem("h_ready"), sem("var_ready"), sem("rstd_ready")
        z_ready, zt_psum, v_psum, q_psum = sem("z_ready"), sem("zt_psum"), sem("v_psum"), sem("q_psum")
        l0_cat_sb, zt_sb, q_sb, v_ready, pt_sb, z2t_sb = (
            [sem(f"{name}{b}") for b in range(BATCH)]
            for name in ("l0_cat_sb", "zt_sb", "q_sb", "v_ready", "pt_sb", "z2t_sb"))
        score_psum, nmax_ready, probs_ready = sem("score_psum"), sem("nmax_ready"), sem("probs_ready")
        pt_psum, pv_psum = sem("pt_psum"), sem("pv_psum")
        var2_ready, rstd2_ready, z2_ready = sem("var2_ready"), sem("rstd2_ready"), sem("z2_ready")
        z2_stored, z2t_psum, logit_psum = sem("z2_stored"), sem("z2t_psum"), sem("logit_psum")
        gap_ready, egap_ready, member_ready, rank_psum = (sem("gap_ready"), sem("egap_ready"),
                                                          sem("member_ready"), sem("rank_psum"))
        gidx_ready, expert_ready = sem("gidx_ready"), sem("expert_ready")
        in_tile_ready, in_row_ready = sem("in_tile_ready"), sem("in_row_ready")
        payload_ready, table_psum, table_ready = sem("payload_ready"), sem("table_psum"), sem("table_ready")
        comb_ready, comb_psum, comb_sb, init_psum, init_sb = (sem("comb_ready"), sem("comb_psum"), sem("comb_sb"),
                                                              sem("init_psum"), sem("init_sb"))
        w1_high_ready, w1_0_low_ready, w1_1_ready = sem("w1_high_ready"), sem("w1_0_low_ready"), sem("w1_1_ready")
        x_high, table_loaded = sem("x_high"), sem("table_loaded")
        b1_cleared, b1_in, b1_ready = sem("b1_cleared"), sem("b1_in"), sem("b1_ready")
        out_stored = sem("out_stored")
        column_ready, scatter_column_ready = sem("column_ready"), sem("scatter_column_ready")
        xt_psum, xt_copied = sem("xt_psum"), sem("xt_copied")
        gather_done = [sem(f"gather_done{i}") for i in range(2)]
        up_psum, gelu_done, ht_psum, ht_act, ht_dve = (sem("up_psum"), sem("gelu_done"), sem("ht_psum"),
                                                       sem("ht_act"), sem("ht_dve"))
        y_psum, y_free, ys_free, y_ready = sem("y_psum"), sem("y_free"), sem("ys_free"), sem("y_ready")
        scatter_done, pool_mark = sem("scatter_done"), sem("pool_mark")

        pieces = [(2, START[2], PATCHES[2], 0)]
        pieces += [(1, START[1] + 512 * i, 512, 1 + i) for i in range(PATCHES[1] // 512)]
        pieces += [(0, START[0] + 512 * i, 512, 3 + i // 2) for i in range(PATCHES[0] // 512)]
        piece_span = [(0, START[1]), (START[1], START[1] + 512), (START[1] + 512, START[0])]
        piece_span += [(START[0] + 1024 * i, START[0] + 1024 * (i + 1)) for i in range(PATCHES[0] // 1024)]

        def image(b):
            return slice(SEQ * b, SEQ * (b + 1))

        block = ctx.enter_context(nc.Block())

        def load_embedding(engine, level):
            highs, f = GATHER_ROWS // FEATURES[level], FEATURES[level]
            src = we[level].rearrange("f g e -> f (g e)")
            for b in range(BATCH):
                dst = we_sb[B1 * b:B1 * b + GATHER_ROWS, level, :, :].rearrange("r g e -> r (g e)")
                engine.dma_start(dst, src if highs == 1 else src[None, :, :].to_broadcast(
                    [highs, f, GROUP * EMBED])).then_inc(we_in[level], 16)

        @block.sync
        def _(sp):
            def load_picks(n):
                lo, hi = piece_span[n]
                sp.dma_start(picks[:, lo:hi], idx[lo:hi].partition_broadcast(P)).then_inc(pick_in[n], 16)

            for n, level in enumerate((2, 1, 0)):
                at = slice(2 * level, 2 * level + 2)
                sp.dma_start(xtab[:, at, :], xt[:, at, :]).then_inc(x_in[level], 16)
                load_picks(n)
            load_picks(3)
            load_embedding(sp, 0)
            load_picks(4)
            sp.dma_start(K[:, K_IDENT:K_END], consts[:, K_IDENT:K_END]).then_inc(kmat_in, 16)
            for n in range(5, 7):
                load_picks(n)
            sp.dma_start(attn0[:, :], attn[0:C0, :]).then_inc(attn_in, 16)
            sp.dma_start(attn1[:, :], attn[C0:MODEL + 1, :]).then_inc(attn_in, 16)
            for b in range(BATCH):
                sp.dma_start(fuse_sb[B1 * b:B1 * b + EMBED, :], fuse).then_inc(wf_in, 16)
            sp.dma_start(bf_sb[:, :], bf.partition_broadcast(P)).then_inc(wf_in, 16)
            sp.dma_start(b2_sb[:, :], b2).then_inc(misc_in, 16)
            sp.wait_ge(b1_cleared, 1)
            for n in range(2):
                for part in range(2):
                    row = 64 * n + 32 * part
                    sp.dma_start(b1_raw[row:row + EXPERTS, :], b1[:, n * NH:(n + 1) * NH]).then_inc(b1_in, 16)
            for e in range(0, EXPERTS, 2):
                w1e = w1[e:e + 2, :, :].rearrange("e c f -> c e f")
                at = slice(e * HIDDEN, (e + 2) * HIDDEN)
                for dst, rows in ((w1_0_raw[:, at], slice(0, C0)), (w1_1_raw[0:C1, at], slice(C0, MODEL)),
                                  (w1_1_raw[C1:P, at], slice(C0, MODEL))):
                    sp.dma_start(dst.rearrange("p (e f) -> p e f", e=2), w1e[rows, :, :]).then_inc(w1_in[e // 2], 16)
            for e in range(0, EXPERTS, 2):
                sp.dma_start(w2_sb[:, e * FK * MODEL:(e + 2) * FK * MODEL].rearrange("p (k c) -> p k c", c=MODEL),
                             w2[e:e + 2, :, :].rearrange("e (k p) c -> p (e k) c", p=P)).then_inc(w2_in, 16)
            for t in range(TOKEN_TILES):
                sp.wait_ge(z2_ready, t + 1)
                rows = slice(t * P, (t + 1) * P)
                sp.dma_start(z2_dram[rows, 0:MODEL], z2[:, t, :]).then_inc(z2_stored, 16)
                sp.dma_start(z2_dram[rows, MODEL:XG], z2[:, t, C0:MODEL]).then_inc(z2_stored, 16)
            for b in range(BATCH):
                sp.wait_ge(init_sb, b + 1)
                sp.dma_start(out.rearrange("(t p) c -> p t c", p=P)[:, 2 * b:2 * b + 2, :],
                             out_init[:, 2 * b:2 * b + 2, :]).then_inc(out_stored, 16)
            sp.wait_ge(out_stored, 16 * BATCH)

        @block.gpsimd
        def _(pool):
            load_embedding(pool, 2)
            load_embedding(pool, 1)
            pool.wait_ge(kmat_in, 16)
            nc.gpsimd.tensor_copy(tri_b[:, :], tri).then_inc(gp_set, 1)
            minus_half = K[:, K_HALF:K_HALF + 2]

            def inverse_root(b, variance, done):
                pool.wait_ge(variance, b + 1)
                nc.gpsimd.tensor_tensor(rstd[:, 2 * b:2 * b + 2], vareps[:, 2 * b:2 * b + 2], minus_half,
                                        ALU.pow).then_inc(done, 1)

            for b in range(BATCH):
                inverse_root(b, var_ready, rstd_ready)

            def split_low(experts):
                for e in experts:
                    pool.wait_ge(w1_high_ready, e + 1)
                    at = slice(e * HIDDEN, (e + 1) * HIDDEN)
                    nc.gpsimd.tensor_tensor(w1_0_low[:, at], w1_0_raw[:, at], w1_0_high[:, at].bitcast(F),
                                            ALU.subtract).then_inc(w1_0_low_ready, 1)

            split_low(range(0, 6))
            for b in range(BATCH):
                inverse_root(b, var2_ready, rstd2_ready)
            split_low(range(6, EXPERTS))

            def gather_column(j, par):
                nc.gpsimd.tensor_copy(gi_col[par][:, :], gidx[:, bass.ds(j, 1)]).then_inc(column_ready, 1)

            def gather(par):
                nc.gpsimd.indirect_dma_start(
                    out=xg[par][:, :], out_offset=None, in_=z2_dram,
                    in_offset=bass.IndirectOffsetOnAxis(gi_col[par][:, 0:1].bitcast(U32), 0)
                ).then_inc(gather_done[par], 16)

            def scatter_column(j, par):
                nc.gpsimd.tensor_copy(si_col[par][:, :], sidx[:, bass.ds(j, 1)]).then_inc(scatter_column_ready, 1)

            def scatter(par):
                nc.gpsimd.indirect_dma_start(
                    out=out, out_offset=bass.IndirectOffsetOnAxis(si_col[par][:, 0:1].bitcast(U32), 0),
                    in_=ys[par][:, :], in_offset=None, bounds_check=TOKENS - 1, oob_is_err=False,
                    compute_op=ALU.add).then_inc(scatter_done, 16)

            def waited():
                pool.sem_inc(pool_mark, 1)

            pool.wait_ge(in_tile_ready, 1)
            nc.gpsimd.tensor_tensor(
                payload[:, :, :, :], in_tile[:, :, None, :].to_broadcast([P, 8, 3, TABLE]),
                values[:, :, :, None].to_broadcast([P, 8, 3, TABLE]), ALU.mult).then_inc(payload_ready, 1)
            pool.wait_ge(z2_stored, 16 * 2 * TOKEN_TILES)
            for j in range(AHEAD):
                if j >= 2:
                    pool.wait_ge(gidx_ready, 1)
                    pool.wait_ge(xt_psum, j - 1)
                    gather_column(j, j % 2)
                pool.wait_ge(column_ready, j + 1)
                gather(j % 2)
            pool.sem_inc(ys_free, 2)
            pool.wait_ge(expert_ready, 1)
            used = pool.value_load(tiles_used[0:1, 0:1], min_val=2 * TOKENS // P, max_val=SLOT_TILES)
            pool.wait_ge(table_ready, 1)
            pool.wait_ge(out_stored, 16 * BATCH)
            with pool.Fori(0, (SLOT_TILES + 1) // 2) as i:
                for par in range(2):
                    j = 2 * i + par
                    with pool.If(j < used):
                        scatter_column(j, par)
                        pool.wait_ge(scatter_column_ready, j + 1)
                        waited()
                        pool.wait_ge(y_ready, j + 1)
                        waited()
                        scatter(par)
                        with pool.If(j + AHEAD - 1 < used):
                            gather_column(j + AHEAD, par)
                            pool.wait_ge(column_ready, j + AHEAD + 1)
                            waited()
                            pool.wait_ge(xt_psum, j + AHEAD - 1)
                            waited()
                            gather(par)
                            waited()
                        with pool.If(j + 1 < used):
                            pool.wait_ge(scatter_done, 16 * j + 16)
                            pool.sem_inc(ys_free, 1)
                        pool.nop()
            pool.wait_ge(scatter_done, 16 * used)
            waited()
            pool.wait_ge(gather_done[0], 16 * (used // 2) + 16)
            waited()
            pool.wait_ge(gather_done[1], 16 * ((used + 1) // 2))
            waited()

        @block.scalar
        def _(act):
            act.dma_start(K[:, 0:K_IDENT], consts[:, 0:K_IDENT]).then_inc(k_in, 16)
            act.wait_ge(k_in, 16)
            nc.scalar.activation(egap[:, :], K[:, K_HALF:K_HALF + TOKEN_TILES], ACT.Exp).then_inc(table_loaded, 1)
            for n, (rows, col, k) in enumerate(((LEVEL_TOKENS[2], EMBED, 1), (LEVEL_TOKENS[1], 0, 0))):
                act.wait_ge(tok_psum, n + 1)
                for b in range(BATCH):
                    r = slice(B1 * b, B1 * b + rows)
                    nc.scalar.copy(t12[r, k, :], bank[2 + b][r, col:col + EMBED]).then_inc(tok_sb, 1)
            act.wait_ge(wf_in, 16 * 3)
            for level in (2, 1):
                act.wait_ge(cat_psum, 3 - level)
                nc.scalar.activation(cat[:, level, :], bank[5 + level][:, 0:SEQ], ACT.Identity,
                                     bias=ebias[:, level:level + 1]).then_inc(cat_sb, 1)
            act.wait_ge(cat_psum, 3)
            nc.scalar.activation(cat[0:EMBED, 0, :], bank[4][0:EMBED, 0:SEQ], ACT.Identity,
                                 bias=ebias[0:EMBED, 0:1]).then_inc(l0_cat_sb[0], 1)

            def split_high(experts):
                for e in experts:
                    act.wait_ge(w1_in[e // 2], 16 * 3)
                    at = slice(e * HIDDEN, (e + 1) * HIDDEN)
                    if e >= 3:
                        act.wait_ge(w1_1_ready, e - 2)
                    nc.scalar.copy(w1_1_high[:, e % 3, :], w1_1_raw[:, at])
                    nc.scalar.copy(w1_0_high[:, at], w1_0_raw[:, at]).then_inc(w1_high_ready, 1)

            split_high(range(0, 3))
            act.wait_ge(qk_psum, 1)
            nc.scalar.mul(qk0[:, :], bank[6][0:C0, 256:257 + MODEL], float(MODEL) ** -0.5).then_inc(qk_sb, 1)
            nc.scalar.mul(qk1[:, :], bank[7][0:C1 + 1, 256:257 + MODEL], float(MODEL) ** -0.5).then_inc(qk_sb, 1)
            act.wait_ge(zt_psum, 1)
            nc.scalar.copy(zt0[:, image(0)], bank[2][:, 0:SEQ])
            nc.scalar.copy(zt1[0:C1, image(0)], bank[2][0:C1, SEQ:2 * SEQ]).then_inc(zt_sb[0], 1)
            split_high(range(3, 4))
            act.wait_ge(q_psum, 1)
            nc.scalar.copy(qt0[:, image(0)], bank[6][:, 0:SEQ])
            nc.scalar.copy(qt1[:, image(0)], bank[6][0:C1 + 1, SEQ:2 * SEQ]).then_inc(q_sb[0], 1)
            act.wait_ge(v_psum, 1)
            nc.scalar.copy(v_sb[:, 0:2, :], bank[4][:, 0:2 * MODEL]).then_inc(v_ready[0], 1)
            split_high(range(4, 5))
            for t in range(TOKEN_TILES):
                act.wait_ge(nmax_ready, t // 2 + 1)
                nc.scalar.activation(probs[:, t, :], bank[t // 2][:, SEQ * (t % 2):SEQ * (t % 2 + 1)], ACT.Exp,
                                     bias=nmax[:, t:t + 1], accum_out=esum[:, t:t + 1]).then_inc(probs_ready, 1)
                if t == 1:
                    split_high(range(5, 6))
            act.wait_ge(pt_psum, 2)
            nc.scalar.copy(probs_t[:, 2:4, :, :], bank[3][:, :]).then_inc(pt_sb[1], 1)
            split_high(range(6, 8))
            act.wait_ge(z2t_psum, 1)
            nc.scalar.copy(z2t0[:, image(0)], bank[6][:, 0:SEQ])
            nc.scalar.copy(z2t1[:, image(0)], bank[6][0:C1, SEQ:2 * SEQ]).then_inc(z2t_sb[0], 1)
            act.wait_ge(gap_ready, 1)
            nc.scalar.activation(egap[:, :], gap[:, :], ACT.Exp).then_inc(egap_ready, 1)
            act.wait_ge(comb_psum, 1)
            nc.scalar.copy(comb_t[:, :], bank[1][0:EXPERTS, :]).then_inc(comb_sb, 1)

            def gelu(par, products):
                for n in range(2):
                    act.wait_ge(up_psum, products + n + 1)
                    last = nc.scalar.activation(hid[:, n * NH:(n + 1) * NH], bank[2 * par + n][:, 0:NH], ACT.Gelu)
                last.then_inc(gelu_done, 1)

            gelu(0, 0)
            act.wait_ge(expert_ready, 1)
            used = act.value_load(tiles_used[0:1, 0:1], min_val=2 * TOKENS // P, max_val=SLOT_TILES)
            with act.Fori(0, (SLOT_TILES + 1) // 2) as i:
                for par in range(2):
                    j = 2 * i + par
                    with act.If(j < used):
                        act.wait_ge(ht_psum, j + 1)
                        nc.scalar.copy(hid_t[:, 0:FK // 2, :], bank[4][:, 0:NH]).then_inc(ht_act, 1)
                        with act.If(j + 1 < used):
                            gelu(1 - par, 2 * j + 2)
                        act.nop()

        @block.vector
        def _(dve):
            chain = [0]

            def link(ins):
                chain[0] += 1
                ins.then_inc(dv, 1)
                dve.wait_ge(dv, chain[0])

            nc.vector.memset(ones_b[:, :], 1.0).then_inc(ones_ready, 1)
            nc.vector.memset(zt1[C1:C1 + 1, :], 1.0).then_inc(gp_set, 1)
            nc.vector.memset(b1_raw[:, :], 0.0).then_inc(b1_cleared, 1)
            nc.vector.memset(ones8[:, :], 1.0).then_inc(gp_set, 1)

            def split_table(level):
                at = slice(2 * level, 2 * level + 2)
                dve.wait_ge(x_in[level], 16)
                link(nc.vector.tensor_copy(xtab_hi[:, at, :], xtab[:, at, :]))
                nc.vector.tensor_tensor(xtab_lo[:, at, :], xtab[:, at, :], xtab_hi[:, at, :].bitcast(F),
                                        ALU.subtract).then_inc(xtab_ready, 1)

            split_table(2)
            dve.wait_ge(k_in, 16)

            def make_onehot(n):
                level, col, width, piece = pieces[n]
                dve.wait_ge(pick_in[piece], 16)
                if n >= 2:
                    dve.wait_ge(picked_psum, n - 1)
                for k in range(2):
                    nc.vector.tensor_scalar(onehot[:, n % 2, k, 0:width], pick_bytes[:, col:col + width, 0],
                                            K[:, K_LOW + k:K_LOW + k + 1], None,
                                            ALU.is_equal).then_inc(onehot_ready, 1)

            def mask_high(n):
                level, col, width, piece = pieces[n]
                dve.wait_ge(picked_psum, n + 1)
                nc.vector.scalar_tensor_tensor(
                    out=gathered[0:ROWS, col:col + width], in0=pick_bytes[0:ROWS, col:col + width, 1],
                    scalar=K[0:ROWS, K_HIGH + level:K_HIGH + level + 1], in1=bank[n % 2][0:ROWS, 0:width],
                    op0=ALU.is_equal, op1=ALU.mult).then_inc(picked_sb, 1)

            make_onehot(0)
            split_table(1)
            for n in range(1, len(pieces)):
                make_onehot(n)
                mask_high(n - 1)
                if n == 1:
                    split_table(0)
            mask_high(len(pieces) - 1)

            dve.wait_ge(b1_in, 16 * 4)
            link(nc.vector.tensor_copy(b1_rows[:, :], b1_raw[:, :]))
            for row in (32, 96):
                last = nc.vector.tensor_tensor(b1_rows[row:row + 32, :], b1_raw[row:row + 32, :],
                                               b1_rows[row:row + 32, :].bitcast(F), ALU.subtract)
            last.then_inc(b1_ready, 1)
            dve.wait_ge(wf_in, 16 * 3)
            dve.wait_ge(cat_psum, 3)
            r = slice(B1, B1 + EMBED)
            nc.vector.tensor_scalar(cat[r, 0, :], bank[5][r, 0:SEQ], ebias[r, 0:1], None,
                                    ALU.add).then_inc(l0_cat_sb[1], 1)

            def statistics(src, b, ready):
                for t in range(2 * b, 2 * b + 2):
                    last = nc.vector.bn_stats(stats[:, t, :], src[:, t, :])
                link(last)
                for t in range(2 * b, 2 * b + 2):
                    last = nc.vector.bn_aggr(mv[:, t, :], stats[:, t, :])
                link(last)
                nc.vector.tensor_scalar(vareps[:, 2 * b:2 * b + 2], mv[:, 2 * b:2 * b + 2, 1], EPS, None,
                                        ALU.add).then_inc(ready, 1)

            def normalize(src, b, rstd_done, dst, done):
                dve.wait_ge(rstd_done, b + 1)
                for t in range(2 * b, 2 * b + 2):
                    nc.vector.tensor_scalar(dst[:, t, :], src[:, t, :], mv[:, t, 0:1], rstd[:, t:t + 1],
                                            ALU.subtract, ALU.mult).then_inc(done, 1)

            for b in range(BATCH):
                dve.wait_ge(h_psum, b + 1)
                for t in range(2 * b, 2 * b + 2):
                    last = nc.vector.tensor_tensor(h[:, t, :], bank[t][:, 0:MODEL], bf_sb[:, :], ALU.add)
                link(last)
                statistics(h, b, var_ready)
            for b in range(BATCH):
                normalize(h, b, rstd_ready, z, z_ready)
            dve.wait_ge(gp_set, 3)

            def split_narrow(experts):
                for e in experts:
                    at = slice(e * HIDDEN, (e + 1) * HIDDEN)
                    dve.wait_ge(w1_high_ready, e + 1)
                    nc.vector.scalar_tensor_tensor(
                        out=w1_1[:, at], in0=w1_1_raw[:, at], scalar=K[:, K_LOWER:K_LOWER + 1],
                        in1=w1_1_high[:, e % 3, :].bitcast(F), op0=ALU.mult, op1=ALU.subtract).then_inc(w1_1_ready, 1)

            split_narrow(range(0, 1))
            dve.wait_ge(zt_psum, 2)
            nc.vector.tensor_copy(zt0[:, image(1)], bank[3][:, 0:SEQ])
            nc.vector.tensor_copy(zt1[0:C1, image(1)], bank[3][0:C1, SEQ:2 * SEQ]).then_inc(zt_sb[1], 1)
            split_narrow(range(1, 4))

            def negative_maximum(b):
                dve.wait_ge(score_psum, b + 1)
                nc.vector.tensor_reduce(nmax[:, 2 * b:2 * b + 2], bank[b][:, :].rearrange("p (t k) -> p t k", t=2),
                                        AX.X, ALU.max, negate=True).then_inc(nmax_ready, 1)

            negative_maximum(0)
            dve.wait_ge(q_psum, 2)
            nc.vector.tensor_copy(qt0[:, image(1)], bank[7][:, 0:SEQ])
            nc.vector.tensor_copy(qt1[:, image(1)], bank[7][0:C1 + 1, SEQ:2 * SEQ]).then_inc(q_sb[1], 1)
            split_narrow(range(4, 5))
            dve.wait_ge(v_psum, 2)
            nc.vector.tensor_copy(v_sb[:, 2:4, :], bank[5][:, 0:2 * MODEL]).then_inc(v_ready[1], 1)
            dve.wait_ge(pt_psum, 1)
            nc.vector.tensor_copy(probs_t[:, 0:2, :, :], bank[2][:, :]).then_inc(pt_sb[0], 1)
            negative_maximum(1)
            split_narrow(range(5, 6))
            for b in range(BATCH):
                tiles = slice(2 * b, 2 * b + 2)
                dve.wait_ge(probs_ready, 2 * b + 2)
                link(nc.vector.reciprocal(rsum[:, tiles], esum[:, tiles]))
                dve.wait_ge(pv_psum, b + 1)
                for t in range(2 * b, 2 * b + 2):
                    last = nc.vector.scalar_tensor_tensor(
                        out=h2[:, t, :], in0=bank[4 + b][:, MODEL * (t % 2):MODEL * (t % 2 + 1)],
                        scalar=rsum[:, t:t + 1], in1=h[:, t, :], op0=ALU.mult, op1=ALU.add)
                link(last)
                statistics(h2, b, var2_ready)
                if b == 0:
                    split_narrow(range(6, 7))
            for b in range(BATCH):
                normalize(h2, b, rstd2_ready, z2, z2_ready)
            dve.wait_ge(z2t_psum, 2)
            nc.vector.tensor_copy(z2t0[:, image(1)], bank[7][:, 0:SEQ])
            nc.vector.tensor_copy(z2t1[:, image(1)], bank[7][0:C1, SEQ:2 * SEQ]).then_inc(z2t_sb[1], 1)

            split_narrow(range(7, 8))
            for c in range(2):
                nc.vector.tensor_copy(values[:, 4 * c:4 * c + 4, 0], K[:, K_TOKEN:K_TOKEN + TOKEN_TILES])
            dve.wait_ge(logit_psum, 1)
            link(nc.vector.tensor_copy(logits[:, :, :], bank[0][:, 0:TOKEN_TILES * EXPERTS]))
            for t in range(TOKEN_TILES):
                last = nc.vector.max(top[:, t, :], logits[:, t, :])
            link(last)
            nc.vector.tensor_tensor(gap[:, :], top[:, :, 1], top[:, :, 0], ALU.subtract).then_inc(gap_ready, 1)
            for t in range(TOKEN_TILES):
                last = nc.vector.max_index(topi[:, t, :], top[:, t, :], logits[:, t, :])
            link(last)
            for c in range(2):
                last = nc.vector.tensor_tensor(
                    chosen[:, c, :, :], iota[:, None, 0:EXPERTS].to_broadcast([P, TOKEN_TILES, EXPERTS]),
                    topi[:, :, c:c + 1].to_broadcast([P, TOKEN_TILES, EXPERTS]), ALU.is_equal)
            link(last)
            nc.vector.tensor_tensor(member[:, :, :], chosen[:, 0, :, :], chosen[:, 1, :, :],
                                    ALU.add).then_inc(member_ready, 1)
            dve.wait_ge(egap_ready, 1)
            link(nc.vector.tensor_scalar(eden[:, :], egap[:, :], 1.0, None, ALU.add))
            link(nc.vector.reciprocal(wgt[:, 0, :], eden[:, :]))
            link(nc.vector.tensor_tensor(wgt[:, 1, :], egap[:, :], wgt[:, 0, :], ALU.mult))
            dve.wait_ge(rank_psum, 1)
            for c, dst in ((0, comb), (1, comb2)):
                if c == 1:
                    nc.vector.tensor_scalar(cnti[:, :], bank[4][:, 32:32 + EXPERTS], float(P - 1), None, ALU.add)
                last = nc.vector.tensor_tensor(dst[:, :, :], chosen[:, c, :, :],
                                               wgt[:, c, :, None].to_broadcast([P, TOKEN_TILES, EXPERTS]), ALU.mult)
            link(last)
            nc.vector.tensor_tensor(comb[:, :, :], comb[:, :, :], comb2[:, :, :], ALU.add).then_inc(comb_ready, 1)
            link(nc.vector.tensor_single_scalar(ntile[:, :], cnti[:, :], 7, ALU.logical_shift_right))
            wgt8 = wgt[:, :, :].rearrange("p c t -> p (c t)")
            nc.vector.tensor_tensor_scan(tile_end[:, :], ones8[:, :], ntile[:, :], 0.0, ALU.mult, ALU.add)
            link(nc.vector.tensor_copy(wgt_hi[:, :], wgt8))
            nc.vector.tensor_tensor(base[:, :], tile_end[:, :], ntile[:, :], ALU.subtract)
            link(nc.vector.tensor_copy(values[:, :, 1], wgt_hi[:, :].bitcast(F)))
            nc.vector.scalar_tensor_tensor(
                out=slot[:, :, :], in0=base[:, None, :].to_broadcast([P, TOKEN_TILES, EXPERTS]), scalar=float(P),
                in1=bank[4][:, 0:32].rearrange("p (t e) -> p t e", t=TOKEN_TILES), op0=ALU.mult, op1=ALU.add)
            link(nc.vector.tensor_tensor(values[:, :, 2], wgt8, wgt_hi[:, :].bitcast(F), ALU.subtract))
            link(nc.vector.tensor_tensor(picked[:, :, :, :], chosen[:, :, :, :],
                                         slot[:, None, :, :].to_broadcast([P, 2, TOKEN_TILES, EXPERTS]), ALU.mult))
            with nc.allow_low_precision(reason="one whole number among zeros"):
                link(nc.vector.tensor_reduce(sloti[:, :], picked[:, :, :, :].rearrange("p c t e -> p (c t) e"),
                                             AX.X, ALU.add))
            nc.vector.tensor_single_scalar(slot_tile[:, :], sloti[:, :], 7, ALU.logical_shift_right)
            link(nc.vector.tensor_single_scalar(slot_row[:, :], sloti[:, :], P - 1, ALU.bitwise_and))
            nc.vector.tensor_tensor(in_tile[:, :, :], iota[:, None, 0:TABLE].to_broadcast([P, 8, TABLE]),
                                    slot_tile[:, :, None].to_broadcast([P, 8, TABLE]),
                                    ALU.is_equal).then_inc(in_tile_ready, 1)
            for c in range(0, 2 * TOKEN_TILES, 4):
                nc.vector.tensor_tensor(in_row[:, c:c + 4, :], iota[:, None, :].to_broadcast([P, 4, P]),
                                        slot_row[:, c:c + 4, None].to_broadcast([P, 4, P]),
                                        ALU.is_equal).then_inc(in_row_ready, 1)
            link(nc.vector.tensor_tensor(before[:, :, :], tile_end[:, None, :].to_broadcast([P, TABLE, EXPERTS]),
                                         iota[:, 0:TABLE, None].to_broadcast([P, TABLE, EXPERTS]), ALU.is_le))
            link(nc.vector.tensor_reduce(expertf[:, :], before[:, :, :], AX.X, ALU.add))
            nc.vector.tensor_scalar(expert[:, :], expertf[:, :], float(EXPERTS - 1), None, ALU.min)
            nc.vector.tensor_scalar(is_expert[:, :], expertf[:, :], K[:, K_ROW:K_ROW + 1], None, ALU.is_equal)
            nc.vector.tensor_copy(tiles_used[:, :], tile_end[:, EXPERTS - 1:EXPERTS]).then_inc(expert_ready, 1)
            dve.wait_ge(table_psum, 1)
            token_psum = bank[5][:, 0:TABLE]
            for j in range(2):
                nc.vector.tensor_scalar(gi_col[j][:, :], bank[5][:, j:j + 1], 1.0, 0.0, ALU.subtract,
                                        ALU.max).then_inc(column_ready, 1)
            nc.vector.tensor_scalar(gidx[:, :], token_psum, 1.0, 0.0, ALU.subtract, ALU.max).then_inc(gidx_ready, 1)
            link(nc.vector.tensor_copy(table[:, :, :], bank[5][:, 0:3 * TABLE]))
            nc.vector.tensor_tensor(slot_w[:, :], table[:, 1, :], table[:, 2, :], ALU.add)
            link(nc.vector.tensor_scalar(pad[:, :], table[:, 0, :], 0.0, 8192.0, ALU.is_equal, ALU.mult))
            link(nc.vector.tensor_tensor(sidxf[:, :], table[:, 0, :], pad[:, :], ALU.add))
            nc.vector.tensor_scalar(sidx[:, :], sidxf[:, :], 1.0, None, ALU.subtract).then_inc(table_ready, 1)

            def copy_rows(j, par):
                nc.vector.tensor_copy(pick_b1[par][:, :], is_expert[:, bass.ds(j, 1)].to_broadcast([P, P]))
                nc.vector.tensor_copy(x0_high[par][:, :], bank[6][:, 0:P])
                nc.vector.tensor_scalar(x1_high[par][:, :], bank[6][:, P:2 * P], K[:, K_SIGN:K_SIGN + 1], None,
                                        ALU.mult).then_inc(x_high, 1)
                dve.wait_ge(x_high, j + 1)
                nc.vector.tensor_tensor(x0_low[par][:, :], bank[6][:, 0:P], x0_high[par][:, :].bitcast(F),
                                        ALU.subtract)
                nc.vector.scalar_tensor_tensor(
                    out=x1_low[par][:, :], in0=bank[6][:, P:2 * P], scalar=K[:, K_SIGN:K_SIGN + 1],
                    in1=x1_high[par][:, :].bitcast(F), op0=ALU.mult, op1=ALU.subtract).then_inc(xt_copied, 1)

            dve.wait_ge(xt_psum, 1)
            copy_rows(0, 0)
            for b in range(BATCH):
                dve.wait_ge(init_psum, b + 1)
                nc.vector.tensor_tensor(out_init[:, 2 * b:2 * b + 2, :],
                                        bank[2 + b][:, 0:2 * MODEL].rearrange("p (t c) -> p t c", t=2),
                                        h2[:, 2 * b:2 * b + 2, :], ALU.add).then_inc(init_sb, 1)
            dve.wait_ge(xt_psum, 2)
            copy_rows(1, 1)
            dve.sem_inc(y_free, 1)
            used = dve.value_load(tiles_used[0:1, 0:1], min_val=2 * TOKENS // P, max_val=SLOT_TILES)
            with dve.Fori(0, (SLOT_TILES + 1) // 2) as i:
                for par in range(2):
                    j = 2 * i + par
                    with dve.If(j < used):
                        dve.wait_ge(ht_psum, j + 1)
                        nc.vector.tensor_copy(hid_t[:, FK // 2:FK, :], bank[5][:, 0:NH]).then_inc(ht_dve, 1)
                        with dve.If(j + 1 < used):
                            dve.wait_ge(xt_psum, j + 3)
                            copy_rows(j + 2, par)
                        dve.wait_ge(ys_free, j + 1)
                        dve.wait_ge(y_psum, j + 1)
                        nc.vector.tensor_scalar(ys[par][:, :], bank[7][:, 0:MODEL], slot_w[:, bass.ds(j, 1)], None,
                                                ALU.mult).then_inc(y_ready, 1)
                        dve.wait_ge(y_ready, j + 1)
                        dve.sem_inc(y_free, 1)

        @block.tensor
        def _(pe):
            def keep_warm(n, bank_n):
                for _ in range(n):
                    nc.tensor.matmul(bank[bank_n][:, :], ones_b[:, 0:P], ones_b[:, :], start=True, stop=True)

            pe.wait_ge(ones_ready, 1)
            keep_warm(13, 0)

            def pick(n):
                level, col, width, piece = pieces[n]
                pe.wait_ge(xtab_ready, 3 - level)
                if n >= 2:
                    pe.wait_ge(picked_sb, n - 1)
                for k in range(2):
                    pe.wait_ge(onehot_ready, 2 * n + k + 1)
                    for part, tab in enumerate((xtab_hi, xtab_lo)):
                        last = nc.tensor.matmul(bank[n % 2][0:ROWS, 0:width], tab[:, 2 * level + k, :],
                                                onehot[:, n % 2, k, 0:width],
                                                start=(k == 0 and part == 0), stop=(k == 1 and part == 1))
                last.then_inc(picked_psum, 1)

            def small_level(level, col, groups):
                nt = LEVEL_TOKENS[level]
                for g in groups:
                    for b in range(BATCH):
                        r = slice(B1 * b, B1 * b + GATHER_ROWS)
                        c = START[level] + g * nt
                        last = nc.tensor.matmul(bank[2 + b][B1 * b:B1 * b + nt, col:col + EMBED], gathered[r, c:c + nt],
                                                we_sb[r, level, g, :], start=(g == 0), stop=(g == GROUP - 1))
                return last

            def fine_level(groups):
                for g in groups:
                    for b in range(BATCH):
                        r = slice(B1 * b, B1 * b + GATHER_ROWS)
                        c = START[0] + g * SEQ
                        last = nc.tensor.matmul(bank[4 + b][B1 * b:B1 * b + EMBED, 0:SEQ], we_sb[r, 0, g, :],
                                                gathered[r, c:c + SEQ], start=(g == 0), stop=(g == GROUP - 1))
                return last

            pick(0)
            keep_warm(4, 7)
            for n, (level, col, width, piece) in enumerate(pieces):
                if n + 1 < len(pieces):
                    pick(n + 1)
                pe.wait_ge(picked_sb, n + 1)
                if n in (0, 1, 3):
                    pe.wait_ge(we_in[level], 32)
                if level == 2:
                    small_level(2, EMBED, range(GROUP)).then_inc(tok_psum, 1)
                elif level == 1:
                    if n == 1:
                        pe.wait_ge(tok_sb, 2)
                    last = small_level(1, 0, range(8 * (n - 1), 8 * n))
                    if n == 2:
                        last.then_inc(tok_psum, 1)
                else:
                    last = fine_level(range(2 * (n - 3), 2 * (n - 2)))
                if n == 4:
                    pe.wait_ge(kmat_in, 16)
                    pe.wait_ge(tok_sb, 4)
                    for level_n, (k, col_k) in ((2, (1, K_UP2)), (1, (0, K_UP1))):
                        for b in range(BATCH):
                            r = slice(B1 * b, B1 * b + LEVEL_TOKENS[level_n])
                            last = nc.tensor.matmul(bank[5 + level_n][B1 * b:B1 * (b + 1), 0:SEQ], t12[r, k, :],
                                                    K[r, col_k:col_k + SEQ], start=True, stop=True)
                        last.then_inc(cat_psum, 1)
            last.then_inc(cat_psum, 1)
            pe.wait_ge(wf_in, 16 * 3)
            pe.wait_ge(cat_sb, 2)
            for level in (2, 1, 0):
                for b in range(BATCH):
                    if level == 0:
                        pe.wait_ge(l0_cat_sb[b], 1)
                    r = slice(B1 * b, B1 * b + EMBED)
                    for half in range(2):
                        last = nc.tensor.matmul(bank[2 * b + half][:, 0:MODEL],
                                                cat[r, level, P * half:P * (half + 1)], wf_sb[r, level, :],
                                                start=(level == 2), stop=(level == 0))
                    if level == 0:
                        last.then_inc(h_psum, 1)

            def transposes(b, src, done, bank_n, signal):
                pe.wait_ge(done, 2 * b + 2)
                for half in range(2):
                    t, c = 2 * b + half, P * half
                    nc.tensor.transpose(bank[bank_n][:, c:c + P], src[:, t, 0:C0], ident)
                    last = nc.tensor.transpose(bank[bank_n][0:C1, SEQ + c:SEQ + c + P], src[:, t, C0:MODEL], ident)
                last.then_inc(signal, 1)

            def queries(b):
                pe.wait_ge(qk_sb, 2)
                pe.wait_ge(zt_sb[b], 1)
                for n, cols in enumerate((slice(0, C0), slice(C0, MODEL + 1))):
                    o = bank[6 + b][0:cols.stop - cols.start, SEQ * n:SEQ * (n + 1)]
                    nc.tensor.matmul(o, qk0[:, cols], zt0[:, image(b)], start=True, stop=False)
                    last = nc.tensor.matmul(o, qk1[:, cols], zt1[:, image(b)], start=False, stop=True)
                last.then_inc(q_psum, 1)

            def values_of(b):
                for half in range(2):
                    t = 2 * b + half
                    o = bank[4 + b][:, MODEL * half:MODEL * (half + 1)]
                    nc.tensor.matmul(o, zt0[:, P * t:P * (t + 1)], wv0[:, :], start=True, stop=False)
                    last = nc.tensor.matmul(o, zt1[:, P * t:P * (t + 1)], wv1[:, :], start=False, stop=True)
                last.then_inc(v_psum, 1)

            def scores(b):
                pe.wait_ge(q_sb[b], 1)
                for half in range(2):
                    t = 2 * b + half
                    o = bank[b][:, SEQ * half:SEQ * (half + 1)]
                    nc.tensor.matmul(o, qt0[:, P * t:P * (t + 1)], zt0[:, image(b)], start=True, stop=False)
                    last = nc.tensor.matmul(o, qt1[:, P * t:P * (t + 1)], zt1[:, image(b)], start=False, stop=True)
                last.then_inc(score_psum, 1)

            def probs_transposed(b):
                for half in range(2):
                    t = 2 * b + half
                    pe.wait_ge(probs_ready, t + 1)
                    for k in range(2):
                        c = P * (2 * half + k)
                        last = nc.tensor.transpose(bank[2 + b][:, c:c + P], probs[:, t, P * k:P * (k + 1)], ident)
                last.then_inc(pt_psum, 1)

            def attended(b):
                pe.wait_ge(v_ready[b], 1)
                pe.wait_ge(pt_sb[b], 1)
                for half in range(2):
                    t = 2 * b + half
                    for k in range(2):
                        last = nc.tensor.matmul(bank[4 + b][:, MODEL * half:MODEL * (half + 1)],
                                                probs_t[:, t, k, :], v_sb[:, 2 * b + k, :],
                                                start=(k == 0), stop=(k == 1))
                last.then_inc(pv_psum, 1)

            pe.wait_ge(attn_in, 16 * 2)
            for bank_n, cols in ((6, slice(0, C0)), (7, slice(C0, MODEL + 1))):
                m = cols.stop - cols.start
                for (lhs, rhs), first in (((wq0, wk0), True), ((wq1, wk1), False)):
                    last = nc.tensor.matmul(bank[bank_n][0:m, 256:257 + MODEL], lhs[:, cols], rhs[:, :],
                                            start=first, stop=not first)
            last.then_inc(qk_psum, 1)
            keep_warm(5, 4)
            transposes(0, z, z_ready, 2, zt_psum)
            transposes(1, z, z_ready, 3, zt_psum)
            queries(0)
            values_of(0)
            scores(0)
            queries(1)
            values_of(1)
            probs_transposed(0)
            scores(1)
            attended(0)
            probs_transposed(1)
            attended(1)
            keep_warm(8, 2)

            def logits_of(b):
                pe.wait_ge(z2t_sb[b], 1)
                for t in range(2 * b, 2 * b + 2):
                    o = bank[0][:, EXPERTS * t:EXPERTS * (t + 1)]
                    nc.tensor.matmul(o, z2t0[:, P * t:P * (t + 1)], rw0[:, :], start=True, stop=False)
                    last = nc.tensor.matmul(o, z2t1[:, P * t:P * (t + 1)], rw1[:, :], start=False, stop=True)
                return last

            for b in range(BATCH):
                transposes(b, z2, z2_ready, 6 + b, z2t_psum)
            keep_warm(1, 2)
            for b in range(BATCH):
                last = logits_of(b)
            last.then_inc(logit_psum, 1)
            pe.wait_ge(gp_set, 3)
            keep_warm(5, 2)
            pe.wait_ge(member_ready, 1)
            memb = member[:, :, :].rearrange("p t e -> p (t e)")
            nc.tensor.matmul(bank[4][:, 0:32], tri_b[:, :], memb, start=True, stop=False, skip_group_check=True)
            for t in range(1, TOKEN_TILES):
                nc.tensor.matmul(bank[4][:, EXPERTS * t:32], ones_b[:, 0:P], memb[:, 0:32 - EXPERTS * t],
                                 start=False, stop=False, skip_group_check=True)
            for t in range(TOKEN_TILES):
                last = nc.tensor.matmul(bank[4][:, 32:32 + EXPERTS], ones_b[:, 0:P],
                                        memb[:, EXPERTS * t:EXPERTS * (t + 1)],
                                        start=False, stop=(t == TOKEN_TILES - 1), skip_group_check=True)
            last.then_inc(rank_psum, 1)
            pe.wait_ge(comb_ready, 1)
            for t in range(TOKEN_TILES):
                last = nc.tensor.transpose(bank[1][0:EXPERTS, P * t:P * (t + 1)], comb[:, t, :], ident)
            last.then_inc(comb_psum, 1)
            keep_warm(8, 7)
            pe.wait_ge(payload_ready, 1)
            for c in range(2 * TOKEN_TILES):
                if c % 4 == 0:
                    pe.wait_ge(in_row_ready, c // 4 + 1)
                last = nc.tensor.matmul(bank[5][:, 0:3 * TABLE], in_row[:, c, :],
                                        payload[:, c, :, :].rearrange("p v t -> p (v t)"),
                                        start=(c == 0), stop=(c == 2 * TOKEN_TILES - 1))
            last.then_inc(table_psum, 1)
            keep_warm(8, 7)
            pe.wait_ge(expert_ready, 1)
            used = pe.value_load(tiles_used[0:1, 0:1], min_val=2 * TOKENS // P, max_val=SLOT_TILES)
            expert_of = [pe.alloc_register(f"expert_of_{par}") for par in range(2)]
            for par in range(2):
                pe.reg_load(expert_of[par], expert[0:1, par:par + 1])
            pe.wait_ge(misc_in, 16)
            pe.wait_ge(comb_sb, 1)
            for t in range(TOKEN_TILES):
                last = nc.tensor.matmul(bank[2 + t // 2][:, MODEL * (t % 2):MODEL * (t % 2 + 1)],
                                        comb_t[:, P * t:P * (t + 1)], b2_sb[:, :], start=True, stop=True)
                if t % 2:
                    last.then_inc(init_psum, 1)

            def transpose_rows(par):
                nc.tensor.transpose(bank[6][:, 0:P], xg[par][:, 0:C0], ident)
                nc.tensor.transpose(bank[6][:, P:2 * P], xg[par][:, C0:XG], ident).then_inc(xt_psum, 1)

            def up_biases(par):
                for n in range(2):
                    r = slice(64 * n, 64 * n + 32 + EXPERTS)
                    nc.tensor.matmul(bank[2 * par + n][:, 0:NH], pick_b1[par][r, :], b1_rows[r, :],
                                     start=True, stop=False)

            def up(e, par, n, low_parts=None):
                at = bass.ds(e * HIDDEN + n * NH, NH)
                for x, w in ((x0_high, w1_0_high[:, at]), (x1_high, w1_1[:, at]), (x0_high, w1_0_low[:, at]),
                             (x0_low, w1_0_high[:, at]), (x1_low, w1_1[:, at])):
                    if x is x0_low and low_parts:
                        pe.wait_ge(xt_copied, low_parts)
                    last = nc.tensor.matmul(bank[2 * par + n][:, 0:NH], x[par][:, :], w, start=False, stop=x is x1_low)
                last.then_inc(up_psum, 1)

            def expert_value(par):
                return pe.snap(expert_of[par], min_val=0, max_val=EXPERTS - 1)

            def transpose_hidden():
                for k in range(FK):
                    c = P * (k % 3)
                    last = nc.tensor.transpose(bank[4 + k // 3][:, c:c + P], hid[:, k * P:(k + 1) * P], ident)
                last.then_inc(ht_psum, 1)

            pe.wait_ge(w2_in, 16 * EXPERTS // 2)
            pe.wait_ge(w1_0_low_ready, EXPERTS)
            pe.wait_ge(b1_ready, 1)
            keep_warm(1, 7)
            pe.wait_ge(gather_done[0], 16)
            transpose_rows(0)
            pe.wait_ge(w1_1_ready, EXPERTS)
            first = expert_value(0)
            pe.wait_ge(x_high, 1)
            up_biases(0)
            up(first, 0, 0, low_parts=1)
            pe.wait_ge(gather_done[1], 16)
            transpose_rows(1)
            up(first, 0, 1)
            pe.wait_ge(init_sb, 2)
            with pe.Fori(0, (SLOT_TILES + 1) // 2) as i:
                for par in range(2):
                    j, other = 2 * i + par, 1 - par
                    with pe.If(j < used):
                        with pe.If(j + 1 < used):
                            nxt = expert_value(other)
                            pe.wait_ge(xt_copied, j + 2)
                            up_biases(other)
                            up(nxt, other, 0)
                            pe.wait_ge(gather_done[par], 16 * i + 32)
                            pe.wait_ge(gelu_done, j + 1)
                            transpose_hidden()
                            transpose_rows(par)
                            up(nxt, other, 1)
                        with pe.Else():
                            pe.wait_ge(gelu_done, j + 1)
                            transpose_hidden()
                        own = expert_value(par)
                        pe.reg_load(expert_of[par], expert[0:1, bass.ds(j + 2, 1)])
                        pe.wait_ge(y_free, j + 1)
                        pe.wait_ge(ht_act, j + 1)
                        pe.wait_ge(ht_dve, j + 1)
                        for k in range(FK):
                            last = nc.tensor.matmul(bank[7][:, 0:MODEL], hid_t[:, k, :],
                                                    w2_sb[:, bass.ds(own * (FK * MODEL) + k * MODEL, MODEL)],
                                                    start=(k == 0), stop=(k == FK - 1))
                        last.then_inc(y_psum, 1)


def kernel(**inputs):
    import concourse.bacc as bacc
    from concourse.bass_utils import run_bass_kernel_spmd

    a = {k: np.asarray(v) for k, v in inputs.items()}
    x = a["x"]

    xt = np.zeros((P, 2 * LEVELS, ROWS), x.dtype)
    for level, p in enumerate((1, 2, 4)):
        side = IMAGE // p
        t = x.reshape(BATCH, CHANNELS, side, p, side, p).transpose(2, 4, 0, 3, 5, 1)
        t = t.reshape(PATCHES[level] // LOW, 2, P, BATCH, FEATURES[level]).transpose(2, 1, 3, 0, 4)
        for b in range(BATCH):
            xt[:, 2 * level:2 * level + 2, B1 * b:B1 * b + GATHER_ROWS] = t[:, :, b].reshape(P, 2, GATHER_ROWS)
    idx = np.concatenate([a[f"L0_tok_idx{level}"].reshape(-1, GROUP).T.reshape(-1) for level in (2, 1, 0)])
    arrays = {"xt": xt, "idx": idx}
    for level in range(LEVELS):
        w = a[f"L0_tok_W{level}"].reshape(EMBED, GROUP, FEATURES[level])
        arrays[f"we{level}"] = w.transpose(2, 1, 0)
    wf = a["L0_tok_Wf"].T.reshape(LEVELS, EMBED, MODEL).transpose(1, 0, 2).reshape(EMBED, LEVELS * MODEL)
    arrays["fuse"] = np.concatenate([wf] + [a[f"L0_tok_b{level}"][:, None] for level in range(LEVELS)], axis=1)
    arrays["bf"] = a["L0_tok_bf"]
    attn = np.zeros((MODEL + 1, A_END), np.float32)
    for col, name in ((A_Q, "q"), (A_K, "k")):
        attn[:MODEL, col:col + MODEL], attn[:MODEL, col + MODEL] = a[f"L0_attn_W{name}"], a[f"L0_attn_b{name}"]
    attn[:MODEL, A_V:A_R], attn[MODEL, A_V:A_R] = a["L0_attn_Wv"].T, a["L0_attn_bv"]
    attn[:MODEL, A_R:] = a["L0_ffn_router_w"].T
    arrays["attn"] = attn
    arrays["w1"], arrays["b1"] = a["L0_ffn_w1"], a["L0_ffn_b1"]
    arrays["w2"], arrays["b2"] = a["L0_ffn_w2"], a["L0_ffn_b2"]

    k = np.zeros((P, K_END), np.float32)
    p = np.arange(P)
    k[:, K_IDENT:K_TRI] = np.eye(P)
    k[:, K_TRI:K_IOTA] = p[:, None] < p[None, :]
    k[:, K_IOTA:K_UP1] = p[None, :]
    for level, col in ((1, K_UP1), (2, K_UP2)):
        n = LEVEL_TOKENS[level]
        pos = np.clip((np.arange(SEQ, dtype=np.float32) + 0.5) * (n / SEQ) - 0.5, 0.0, n - 1)
        lo = np.floor(pos).astype(int)
        hi = np.minimum(lo + 1, n - 1)
        up = np.zeros((n, SEQ), np.float32)
        np.add.at(up, (lo, np.arange(SEQ)), 1.0 - (pos - lo))
        np.add.at(up, (hi, np.arange(SEQ)), pos - lo)
        k[:n, col:col + SEQ] = k[B1:B1 + n, col:col + SEQ] = up
    k[:, K_LOW], k[:, K_LOW + 1] = p, p + P
    for level in range(LEVELS):
        k[:, K_HIGH + level] = (p % B1) // FEATURES[level]
    for t in range(TOKEN_TILES):
        k[:, K_TOKEN + t] = t * P + p + 1
    k[:, K_HALF:K_ROW] = -0.5
    k[:, K_ROW] = p % 32
    k[:, K_LOWER] = p >= C1
    k[:, K_SIGN] = np.where(p < C1, -1, 1)
    arrays["consts"] = k

    nc = bacc.Bacc("TRN2", target_bir_lowering=False, num_devices=1)
    aps, feeds = {}, {}
    for name, array in arrays.items():
        array = np.ascontiguousarray(array)
        feeds[f"in_{name}"] = array
        aps[name] = nc.dram_tensor(f"in_{name}", array.shape, mybir.dt.from_np(array.dtype), kind="ExternalInput").ap()
    out = nc.dram_tensor("out", (TOKENS, MODEL), mybir.dt.float32, kind="ExternalOutput").ap()
    build(nc, aps["xt"], aps["idx"], [aps[f"we{level}"] for level in range(LEVELS)], aps["fuse"], aps["bf"],
          aps["attn"], aps["w1"], aps["b1"], aps["w2"], aps["b2"], aps["consts"], out)
    result = run_bass_kernel_spmd(nc, [feeds], core_ids=[0])
    return result.results[0]["out"].reshape(BATCH, SEQ, MODEL)
```
